# Optimizing a Trainium2 kernel written in Bass

```python
import numpy as np
import jax
import jax.numpy as jnp

def _softmax(x, axis=-1):
    return jax.nn.softmax(x, axis=axis)

def _gelu(x):
    return jax.nn.gelu(x, approximate=True)

def _silu(x):
    return jax.nn.silu(x)

def _sigmoid(x):
    return jax.nn.sigmoid(x)

def _layernorm(x, axis=-1, eps=1e-05):
    m = jnp.mean(x, axis=axis, keepdims=True)
    v = jnp.var(x, axis=axis, keepdims=True)
    return (x - m) / jnp.sqrt(v + eps)

def _scatter_add(tgt, idx, src, axis=0):
    return tgt.at[idx].add(src)

def _segment_sum(src, seg, n):
    return jax.ops.segment_sum(src, seg, n)
kernel_name = 'mk_gnn_preln_d4_gnn_r32_eca668'

def setup_inputs(seed: int=0):
    np.random.seed(seed)
    _w = jnp.asarray

    def _rec_inputs():
        import jax
        import jax.numpy as jnp
        _gk = jax.random.key(seed)
        x = -0.0003713 + 1 * jax.random.normal(jax.random.fold_in(_gk, 1), (3125, 256), jnp.float32)
        _s = jax.random.randint(jax.random.fold_in(_gk, 2), (25000,), 0, 3125, jnp.int32)
        _d = jax.random.randint(jax.random.fold_in(_gk, 3), (25000,), 0, 3125, jnp.int32)
        _loop = jnp.arange(3125, dtype=jnp.int32)
        src = jnp.concatenate([_s, _d, _loop])
        dst = jnp.concatenate([_d, _s, _loop])
        _o = jnp.argsort(dst, stable=True)
        src = src[_o]
        dst = dst[_o]
        edge_type_8 = jax.random.randint(jax.random.fold_in(_gk, 13), (53125,), 0, 8, jnp.int32)
        edge_weight = jax.random.uniform(jax.random.fold_in(_gk, 14), (53125,), jnp.float32, 0.0, 0.999998)
        return (x, src, dst, edge_type_8, edge_weight)
    x, src, dst, edge_type_8, edge_weight = _rec_inputs()

    def _L0_gnn_setup():
        import jax, jax.numpy as jnp
        import numpy as np
        NUM_NODES = 50000
        NUM_EDGES = 25000
        IN_DIM = 256
        OUT_DIM = 256
        NUM_RELATIONS = 8
        key = jax.random.key(seed)
        k1, k2, k3, k4 = jax.random.split(key, 4)
        node_repr = jax.random.normal(k1, (NUM_NODES, IN_DIM), dtype=jnp.float32)
        edge_index = jax.random.randint(k2, (2, NUM_EDGES), 0, NUM_NODES, dtype=jnp.int64)
        edge_types = jax.random.randint(k3, (NUM_EDGES,), 0, NUM_RELATIONS, dtype=jnp.int64)
        limit = float(np.sqrt(6.0 / (IN_DIM + OUT_DIM)))
        weight = jax.random.uniform(k4, (NUM_RELATIONS, OUT_DIM, IN_DIM), dtype=jnp.float32, minval=-limit, maxval=limit)
        bias = jnp.zeros((OUT_DIM,), dtype=jnp.float32)
        return {'node_repr': node_repr, 'weight': weight, 'bias': bias, 'edge_index': edge_index, 'edge_types': edge_types}
    _L0_gnn_all = _L0_gnn_setup()
    _L0_gnn_in = {k: v for k, v in _L0_gnn_all.items() if k in ('weight', 'bias')}
    del _L0_gnn_all

    def _L1_gnn_setup():
        import jax, jax.numpy as jnp
        import numpy as np
        N_NODES = 50000
        N_EDGES = 25000
        IN_F = 256
        OUT_F = 64
        HEADS = 4
        NEG_SLOPE = 0.2
        key = jax.random.key(seed)
        ks = jax.random.split(key, 6)
        x = jax.random.normal(ks[0], (N_NODES, IN_F), dtype=jnp.float32)
        edge_index = jax.random.randint(ks[1], (2, N_EDGES), 0, N_NODES, dtype=jnp.int32)
        edge_weight = jax.random.uniform(ks[2], (N_EDGES,), dtype=jnp.float32)
        gain = float(np.sqrt(2.0 / (1.0 + NEG_SLOPE ** 2)))
        w_bound = gain * np.sqrt(6.0 / (IN_F + OUT_F))
        a_bound = gain * np.sqrt(6.0 / (OUT_F + 1))
        W = jax.random.uniform(ks[3], (HEADS, IN_F, OUT_F), minval=-w_bound, maxval=w_bound, dtype=jnp.float32)
        a_src = jax.random.uniform(ks[4], (HEADS, OUT_F, 1), minval=-a_bound, maxval=a_bound, dtype=jnp.float32)
        a_dst = jax.random.uniform(ks[5], (HEADS, OUT_F, 1), minval=-a_bound, maxval=a_bound, dtype=jnp.float32)
        return {'x': x, 'edge_index': edge_index, 'edge_weight': edge_weight, 'W': W, 'a_src': a_src, 'a_dst': a_dst}
    _L1_gnn_all = _L1_gnn_setup()
    _L1_gnn_in = {k: v for k, v in _L1_gnn_all.items() if k in ('W', 'a_src', 'a_dst')}
    del _L1_gnn_all

    def _L2_gnn_setup():
        import jax, jax.numpy as jnp
        import numpy as np
        N_NODES = 3125
        N_EDGES = 100000
        D_IN = 256
        D_OUT = 256
        key = jax.random.key(seed)
        k1, k2, k3, k4, k5, k6 = jax.random.split(key, 6)
        x = jax.random.normal(k1, (N_NODES, D_IN), dtype=jnp.float32)
        edge_val = jax.random.uniform(k2, (N_EDGES,), dtype=jnp.float32)
        stdv = 1.0 / np.sqrt(D_OUT)
        W = jax.random.uniform(k3, (D_IN, D_OUT), dtype=jnp.float32, minval=-stdv, maxval=stdv)
        b = jax.random.uniform(k4, (D_OUT,), dtype=jnp.float32, minval=-stdv, maxval=stdv)
        edge_row = jax.random.randint(k5, (N_EDGES,), 0, N_NODES, dtype=jnp.int32)
        edge_col = jax.random.randint(k6, (N_EDGES,), 0, N_NODES, dtype=jnp.int32)
        return {'x': x, 'edge_val': edge_val, 'W': W, 'b': b, 'edge_row': edge_row, 'edge_col': edge_col}
    _L2_gnn_all = _L2_gnn_setup()
    _L2_gnn_in = {k: v for k, v in _L2_gnn_all.items() if k in ('W', 'b')}
    del _L2_gnn_all

    def _L3_gnn_setup():
        import jax, jax.numpy as jnp
        import numpy as np
        N, IN_CH, HEADS, OUT_CH, E = (50000, 256, 4, 64, 25000)
        key = jax.random.key(seed)
        k1, k2, k3, k4, k5 = jax.random.split(key, 5)
        x = jax.random.normal(k1, (N, IN_CH), dtype=jnp.float32)
        edge_index = jax.random.randint(k2, (2, E), 0, N, dtype=jnp.int64)
        bw = float(np.sqrt(6.0 / (IN_CH + HEADS * OUT_CH)))
        ba = float(np.sqrt(6.0 / (HEADS + OUT_CH)))
        weight = jax.random.uniform(k3, (IN_CH, HEADS * OUT_CH), jnp.float32, -bw, bw)
        attn_l = jax.random.uniform(k4, (HEADS, OUT_CH), jnp.float32, -ba, ba)
        attn_r = jax.random.uniform(k5, (HEADS, OUT_CH), jnp.float32, -ba, ba)
        return {'x': x, 'edge_index': edge_index, 'weight': weight, 'attn_l': attn_l, 'attn_r': attn_r}
    _L3_gnn_all = _L3_gnn_setup()
    _L3_gnn_in = {k: v for k, v in _L3_gnn_all.items() if k in ('weight', 'attn_l', 'attn_r')}
    del _L3_gnn_all
    return {'x': x, 'src': src, 'dst': dst, 'edge_type_8': edge_type_8, 'edge_weight': edge_weight, 'L0_gnn_weight': _L0_gnn_in['weight'], 'L0_gnn_bias': _L0_gnn_in['bias'], 'L1_gnn_W': _L1_gnn_in['W'], 'L1_gnn_a_src': _L1_gnn_in['a_src'], 'L1_gnn_a_dst': _L1_gnn_in['a_dst'], 'L2_gnn_W': _L2_gnn_in['W'], 'L2_gnn_b': _L2_gnn_in['b'], 'L3_gnn_weight': _L3_gnn_in['weight'], 'L3_gnn_attn_l': _L3_gnn_in['attn_l'], 'L3_gnn_attn_r': _L3_gnn_in['attn_r']}

def reference(x, src, dst, edge_type_8, edge_weight, L0_gnn_weight, L0_gnn_bias, L1_gnn_W, L1_gnn_a_src, L1_gnn_a_dst, L2_gnn_W, L2_gnn_b, L3_gnn_weight, L3_gnn_attn_l, L3_gnn_attn_r):
    import jax
    import jax.numpy as jnp

    def _L0_gnn_ref(node_repr, weight, bias, edge_index, edge_types):
        import jax, jax.numpy as jnp
        import numpy as np
        NUM_NODES = 50000
        NUM_EDGES = 25000
        IN_DIM = 256
        OUT_DIM = 256
        NUM_RELATIONS = 8
        h_all = jnp.einsum('ni,roi->rno', node_repr, weight)
        src, dst = (edge_index[0], edge_index[1])
        msgs = h_all[edge_types, src]
        messages = jax.ops.segment_sum(msgs, dst, num_segments=node_repr.shape[0])
        return messages + bias

    def _L1_gnn_ref(x, edge_index, edge_weight, W, a_src, a_dst):
        import jax, jax.numpy as jnp
        import numpy as np
        N_NODES = 50000
        N_EDGES = 25000
        IN_F = 256
        OUT_F = 64
        HEADS = 4
        NEG_SLOPE = 0.2
        num_nodes = x.shape[0]
        h = jnp.einsum('ni,hio->hno', x, W)
        attn_src = jnp.einsum('hno,hod->hn', h, a_src)
        attn_dst = jnp.einsum('hno,hod->hn', h, a_dst)
        src_idx, dst_idx = (edge_index[0], edge_index[1])
        e = attn_src[:, src_idx] + attn_dst[:, dst_idx]
        e = jnp.where(e >= 0, e, NEG_SLOPE * e)
        e = e * edge_weight[None, :]
        e_exp = jnp.exp(e - jnp.max(e))
        denom = jax.ops.segment_sum(e_exp.T, dst_idx, num_segments=num_nodes).T
        alpha = e_exp / (denom[:, dst_idx] + 1e-10)
        msg = h[:, src_idx] * alpha[..., None]
        out = jax.vmap(lambda m: jax.ops.segment_sum(m, dst_idx, num_segments=num_nodes))(msg)
        return jnp.transpose(out, (1, 0, 2)).reshape(num_nodes, HEADS * OUT_F)

    def _L2_gnn_ref(x, edge_val, W, b, edge_row, edge_col):
        import jax, jax.numpy as jnp
        import numpy as np
        N_NODES = 3125
        N_EDGES = 100000
        D_IN = 256
        D_OUT = 256
        support = jnp.matmul(x, W)
        gathered = support[edge_col] * edge_val[:, None]
        out = jax.ops.segment_sum(gathered, edge_row, num_segments=x.shape[0])
        return out + b

    def _L3_gnn_ref(x, edge_index, weight, attn_l, attn_r):
        import jax, jax.numpy as jnp
        import numpy as np
        N, IN_CH, HEADS, OUT_CH, E = (50000, 256, 4, 64, 25000)
        heads, out_ch = attn_l.shape
        n = x.shape[0]
        xt = jnp.matmul(x, weight).reshape(-1, heads, out_ch)
        row, col = (edge_index[0], edge_index[1])
        alpha_l = jnp.einsum('ehd,hd->eh', xt[row], attn_l)
        alpha_r = jnp.einsum('ehd,hd->eh', xt[col], attn_r)
        alpha = jax.nn.softmax(jax.nn.leaky_relu(alpha_l + alpha_r, 0.01), axis=1)
        tmp = jnp.einsum('nh,nhd->nd', alpha[:n], xt[col[:n]])
        out = jnp.broadcast_to(tmp[:, None, :], (n, heads, out_ch))
        return out.reshape(n, heads * out_ch)
    edge_index = jnp.stack([src, dst])
    h = jnp.maximum(_layernorm(x, axis=-1), 0.0)
    x = x + _L0_gnn_ref(h, L0_gnn_weight, L0_gnn_bias, edge_index, edge_type_8)
    h = jnp.maximum(_layernorm(x, axis=-1), 0.0)
    x = x + _L1_gnn_ref(h, edge_index, edge_weight, L1_gnn_W, L1_gnn_a_src, L1_gnn_a_dst)
    h = jnp.maximum(_layernorm(x, axis=-1), 0.0)
    x = x + _L2_gnn_ref(h, edge_weight, L2_gnn_W, L2_gnn_b, src, dst)
    h = jnp.maximum(_layernorm(x, axis=-1), 0.0)
    x = x + _L3_gnn_ref(h, edge_index, L3_gnn_weight, L3_gnn_attn_l, L3_gnn_attn_r)
    return x

_drawn_inputs = setup_inputs


def setup_inputs(seed=0):
    import zlib

    import numpy as np

    out = dict(_drawn_inputs(seed))
    spreads = {'L0_gnn_bias': (0.0, 0.288)}
    factors = {'L2_gnn_b': 7.964}
    for name, (base, spread) in spreads.items():
        noise = np.random.default_rng([zlib.crc32(name.encode()), seed]).standard_normal(out[name].shape)
        drawn = base * np.exp(spread * noise) if base else spread * noise
        out[name] = jnp.asarray(drawn.astype(out[name].dtype))
    for name, factor in factors.items():
        out[name] = (out[name] * factor).astype(out[name].dtype)
    return out
```

```python
from contextlib import ExitStack

import concourse.bass as bass
from concourse import mybir

F32 = mybir.dt.float32
BF16 = mybir.dt.bfloat16
I32 = mybir.dt.int32
ALU = mybir.AluOpType
ACT = mybir.ActivationFunctionType
AX = mybir.AxisListType

P = 128
N, F, E, R, H = 3125, 256, 53125, 8, 4
NB = -(-N // P)
ET = -(-E // P)
NT = ET + NB
BLK = 7
SETS = 3
RING = BLK * SETS
ITERS = NT // RING
assert NT == ITERS * RING
FW = F + 2 * H
RW = F + 8
SH = 8
SITERS = ET // (2 * SH)
assert ET == SITERS * 2 * SH
NG = 5
PITERS = NB // NG
KT = F // P
EPS = 1e-5
FAR = 1e30

C_IOTA, C_ID, C_TRI, C_SLOT, C_PART, C_PAD = 0, P, 2 * P, 3 * P, 3 * P + NT, 3 * P + NT + 1
CW = C_PAD + 1
NEXT = PITERS * NG


def build(nc, x, ecols, wcols, consts, w0, bias0, w1, a1, w2, b2, w3, a3, out):
    with ExitStack() as ctx:
        def sb(name, shape, dt=F32):
            return ctx.enter_context(nc.sbuf_tensor(name, shape, dt))

        def sem(name):
            return ctx.enter_context(nc.semaphore(name))

        def dram(name, shape, dt=F32):
            return nc.dram_tensor(name, shape, dt, kind="Internal").ap()

        table0_rows = dram("table0", [NB * P * R, F])
        table0 = table0_rows.rearrange("(n r) f -> n (r f)", r=R)
        tables = [None, dram("table1", [NB * P, F]), dram("table2", [NB * P, F]), dram("table3", [NB * P, FW])]
        tableL = dram("tableL", [NB * P, H])
        slot_rows = [dram("slots_dst", [P * NT + P, 4]), dram("slots_src", [P * NT + P, 4])]

        X = sb("X", [P, NB, F])
        cst = sb("cst", [P, CW])
        iota, ident = cst[:, C_IOTA:C_IOTA + P], cst[:, C_ID:C_ID + P]
        slot_no, part, pad_row = cst[:, C_SLOT:C_SLOT + NT], cst[:, C_PART:C_PART + 1], cst[:, C_PAD:C_PAD + 1]
        ident_b = sb("ident_b", [P, P], BF16)
        tri_b = sb("tri_b", [P, P], BF16)
        ones_b = sb("ones_b", [P, P], BF16)
        ones_row = sb("ones_row", [P, ET])
        bias0_b = sb("bias0_b", [P, F])
        b2_b = sb("b2_b", [P, F])
        W1 = sb("W1", [P, KT, FW])
        W2 = sb("W2", [P, KT, F])
        W3 = sb("W3", [P, KT, FW])

        ecol = sb("ecol", [P, 3, ET], I32)
        wcol = sb("wcol", [P, ET])
        rec_d = sb("rec_d", [P, NT, 4])
        rec = [rec_d[:, 0:ET, :], sb("rec_s", [P, ET, 4])]
        rank_f = sb("rank_f", [P, ET])
        run = sb("run", [P, ET])
        tmp_i = sb("tmp_i", [P, NT], I32)
        tmp_j = sb("tmp_j", [P, ET], I32)
        place = [sb("place_dst", [P, ET], I32), sb("place_src", [P, ET], I32)]
        total = sb("total", [P, 6, NB])
        total_i = sb("total_i", [P, NB], I32)
        tile_bucket = [sb("tile_bucket_d", [P, NT]), sb("tile_bucket_s", [P, NT])]
        tile_bucket_i = [sb("tile_bucket_di", [P, NT], I32), sb("tile_bucket_si", [P, NT], I32)]
        rec_ring = sb("rec_ring", [P, 2 * SH, 4])
        place_ring = sb("place_ring", [P, 2 * SH], I32)

        slots = [sb("slots_d", [P, NT, 4]), rec_d]
        local = [sb("local_d", [P, NT]), sb("local_s", [P, NT])]
        idx_ring = sb("idx_ring", [P, RING], I32)

        arena = sb("arena", [P, 3 * NB * ET // 2])
        arena_b = arena[:, :].bitcast(BF16)
        member = arena_b[:, 0:NB * ET].rearrange("p (b t) -> p b t", b=NB)
        count = arena_b[:, NB * ET:2 * NB * ET].rearrange("p (b t) -> p b t", b=NB)
        before = arena_b[:, 2 * NB * ET:3 * NB * ET].rearrange("p (b t) -> p b t", b=NB)
        rows = arena[:, 0:RING * RW].rearrange("p (s f) -> p s f", s=RING)
        U = arena[:, RING * RW:RING * RW + NB * (F + H)].rearrange("p (n f) -> p n f", n=NB)
        final_rows = arena[:, 0:NB * FW].rearrange("p (n f) -> p n f", n=NB)
        oh_at = RING * RW + NB * (F + H)
        onehot = arena[:, oh_at:oh_at + RING * P].rearrange("p (k j c) -> p k j c", k=SETS, j=BLK)
        assert oh_at + RING * P <= 3 * NB * ET // 2

        W0 = sb("W0", [P, KT, R * F])
        w0_flat = W0[:, :, :].rearrange("p k c -> p (k c)")
        logit = w0_flat[:, 0:NT * H].rearrange("p (t h) -> p t h", h=H)
        h_ring = sb("h_ring", [P, NG, F])
        hT_ring = sb("hT_ring", [P, NG, KT, P])
        out_ring = sb("out_ring", [P, 4, 2 * F])
        row_ring = sb("row_ring", [P, NG, FW])
        A1, A3, folded = row_ring[:, 1:3, 0:F], row_ring[:, 3:5, 0:F], row_ring[:, 0, 0:F]
        stats = sb("stats", [P, NB, 6])
        mean_var = sb("mean_var", [P, NB, 2])
        rstd = sb("rstd", [P, NB])
        shift = sb("shift", [P, NB])

        attn = sb("attn", [P, NB, 2 * H])
        attn_rest = sb("attn_rest", [P, 2, NB, H])
        attn_part = sb("attn_part", [P, 2, 3, NB, H], BF16)
        lo_b = sb("lo_b", [P, 2, NT], BF16)
        hi_f = sb("hi_f", [P, 2, NT])
        onehotT = sb("onehotT", [P, 2, BLK * P], BF16)
        out_flat = out_ring[:, :, :].rearrange("p q c -> p (q c)")
        picked = out_flat[:, 0:BLK * 2 * NB * H].rearrange("p (j c) -> p j c", j=BLK)
        pick = out_flat[:, BLK * 2 * NB * H:BLK * 2 * NB * (H + 1)].rearrange("p (j s b) -> p j s b", j=BLK, s=2)
        off = sb("off", [P, NT])
        mx = sb("mx", [P, 4])
        mrow = sb("mrow", [1, 4])
        al = sb("al", [P, NB, H])
        sc = sb("sc", [P, NB, H])
        sc2 = sb("sc2", [P, NB, H])
        sm = sb("sm", [P, NB, 2])

        ps = ctx.enter_context(nc.psum_tensor("ps", [P, 8, 512], F32))

        s_in = sem("s_in")
        s_x = sem("s_x")
        s_w = sem("s_w")
        s_prep = sem("s_prep")
        s_constb = sem("s_constb")
        s_member = sem("s_member")
        s_count = sem("s_count")
        s_before = sem("s_before")
        s_count_out = sem("s_count_out")
        s_before_out = sem("s_before_out")
        s_blank = sem("s_blank")
        s_blanked = sem("s_blanked")
        s_place = sem("s_place")
        s_recs = sem("s_recs")
        s_scat = [sem(f"s_scat{h}") for h in range(2)]
        s_slots = [sem("s_slots_d"), sem("s_slots_s")]
        s_local = sem("s_local")
        s_var = sem("s_var")
        s_sd = sem("s_sd")
        s_norm = sem("s_norm")
        s_h = sem("s_h")
        s_tr = sem("s_tr")
        s_hT = sem("s_hT")
        s_quarter = sem("s_quarter")
        s_quarter_out = sem("s_quarter_out")
        s_quarter_free = sem("s_quarter_free")
        s_store0 = [sem(f"s_store0_{q}") for q in range(4)]
        s_row = sem("s_row")
        s_row_out = sem("s_row_out")
        s_row_free = sem("s_row_free")
        s_store = [sem(f"s_store{j}") for j in range(NG)]
        s_storeL = [sem(f"s_storeL{j}") for j in range(NG)]
        s_idx = sem("s_idx")
        s_rows = [sem(f"s_rows{k}") for k in range(SETS)]
        s_onehot = sem("s_onehot")
        s_scaled = sem("s_scaled")
        s_mm = sem("s_mm")
        s_added = sem("s_added")
        s_att = sem("s_att")
        s_bc = sem("s_bc")
        s_ohT = sem("s_ohT")
        s_picks = sem("s_picks")
        s_pd = sem("s_pd")
        s_chainl = sem("s_chainl")
        s_mx = sem("s_mx")
        s_mT = sem("s_mT")
        s_m1 = sem("s_m1")
        s_mB = sem("s_mB")
        s_negM = sem("s_negM")
        s_exp = sem("s_exp")
        s_last = [sem(f"s_last{g}") for g in range(PITERS)]
        s_e3 = sem("s_e3")
        s_e3x = sem("s_e3x")
        s_done = sem("s_done")
        s_out = sem("s_out")
        s_tok_act = sem("s_tok_act")
        s_tok_sp = sem("s_tok_sp")
        s_tok_pool = sem("s_tok_pool")
        s_tok_dve = sem("s_tok_dve")

        def hold(eng, s, value, token):
            eng.wait_ge(s, value)
            eng.sem_inc(token, 1)

        block = ctx.enter_context(nc.Block())

        @block.sync
        def _(sp):
            sp.dma_start(cst[:, :], consts).then_inc(s_in, 16)
            sp.dma_start(ecol[:, :, :], ecols).then_inc(s_in, 16)
            sp.dma_start(wcol[:, :], wcols).then_inc(s_in, 16)
            sp.dma_start(X[:, :, :], x).then_inc(s_x, 16)
            sp.dma_start(W0[:, :, :], w0).then_inc(s_w, 16)
            for dst, src in ((W1[:, :, 0:F], w1), (W2[:, :, :], w2), (W3[:, :, 0:F], w3)):
                sp.dma_start(dst, src).then_inc(s_w, 16)
            for dst, src in ((A1, a1), (A3, a3)):
                sp.dma_start(dst, src.unsqueeze(0).to_broadcast([P, 2, F])).then_inc(s_w, 16)
            for dst, src in ((bias0_b, bias0), (b2_b, b2)):
                sp.dma_start(dst[:, :], src.to_broadcast([P, F])).then_inc(s_w, 16)
            sp.wait_ge(s_blank, 1)
            for q in range(2):
                sp.dma_start(slot_rows[q][0:P * NT, :].rearrange("(p t) c -> p (t c)", p=P),
                             slots[0][:, :, :].rearrange("p t c -> p (t c)")).then_inc(s_blanked, 16)

            def load_slots(q):
                for h in range(2):
                    sp.wait_ge(s_scat[h], (q + 1) * SITERS * SH * 16)
                sp.dma_start(slots[q][:, :, :].rearrange("p t c -> p (t c)"),
                             slot_rows[q][0:P * NT, :].rearrange("(p t) c -> p (t c)", p=P)).then_inc(s_slots[q], 16)

            for q in range(4):
                sp.wait_ge(s_quarter_out, 4 + q + 1)
                sp.dma_start(table0[0:P, q * 2 * F:(q + 1) * 2 * F], out_ring[:, q, :]).then_inc(s_store0[q], 16)
            with sp.Fori(1, NB) as n:
                for q in range(4):
                    sp.wait_ge(s_store0[q], n * 16)
                    sp.sem_inc(s_quarter_free, 1)
                    hold(sp, s_quarter_out, n * 4 + (4 + q + 1), s_tok_sp)
                    sp.dma_start(table0[bass.ds(n * P, P), q * 2 * F:(q + 1) * 2 * F],
                                 out_ring[:, q, :]).then_inc(s_store0[q], 16)
            load_slots(0)

            def store_rows(l):
                def turn(i, first):
                    for j in range(NG):
                        if not (first and l == 1):
                            hold(sp, s_store[j], (i + (l - 1) * PITERS) * 16, s_tok_sp)
                            if l == 3 and not first:
                                hold(sp, s_storeL[j], i * 16, s_tok_sp)
                            sp.sem_inc(s_row_free, 1)
                        hold(sp, s_row_out, (i + (l - 1) * PITERS) * NG + (j + 1 + NG), s_tok_sp)
                        at = i * (NG * P) + j * P
                        wide = FW if l == 3 else F
                        sp.dma_start(tables[l][bass.ds(at, P), :] if not first else tables[l][j * P:(j + 1) * P, :],
                                     row_ring[:, j, 0:wide]).then_inc(s_store[j], 16)
                        if l == 3:
                            sp.dma_start(tableL[bass.ds(at, P), :] if not first else tableL[j * P:(j + 1) * P, :],
                                         row_ring[:, j, F + H:FW]).then_inc(s_storeL[j], 16)
                turn(0, True)
                with sp.Fori(1, PITERS) as i:
                    turn(i, False)

            store_rows(1)
            load_slots(1)
            store_rows(2)
            store_rows(3)
            for g in range(PITERS):
                sp.wait_ge(s_done, g + 1)
                sp.dma_start(out[:, g * NG:(g + 1) * NG, :], X[:, g * NG:(g + 1) * NG, :]).then_inc(s_out, 16)
            sp.wait_ge(s_out, PITERS * 16)

        @block.gpsimd
        def _(pool):
            def scatter(q):
                with pool.Fori(0, SITERS) as i:
                    for h in range(2):
                        hold(pool, s_recs, i * 2 + (q * 2 * SITERS + h + 1), s_tok_pool)
                        for j in range(h * SH, (h + 1) * SH):
                            nc.gpsimd.indirect_dma_start(
                                out=slot_rows[q], out_offset=bass.IndirectOffsetOnAxis(ap=place_ring[:, j:j + 1], axis=0),
                                in_=rec_ring[:, j, :], in_offset=None).then_inc(s_scat[h], 16)

            def gather(l, table):
                with pool.Fori(0, ITERS) as i:
                    for k in range(SETS):
                        hold(pool, s_idx, i * SETS + (l * ITERS * SETS + k + 1), s_tok_pool)
                        for j in range(k * BLK, (k + 1) * BLK):
                            nc.gpsimd.indirect_dma_start(
                                out=rows[:, j, 0:F], out_offset=None, in_=table,
                                in_offset=bass.IndirectOffsetOnAxis(ap=idx_ring[:, j:j + 1], axis=0)).then_inc(s_rows[k], 16)

            pool.wait_ge(s_blanked, 32)
            scatter(0)
            for q in range(4):
                pool.wait_ge(s_store0[q], NB * 16)
            pool.wait_ge(s_place, 2)
            gather(0, table0_rows)
            scatter(1)
            for l in (1, 2):
                for j in range(NG):
                    pool.wait_ge(s_store[j], l * PITERS * 16)
                gather(l, tables[l])
            for j in range(NG):
                pool.wait_ge(s_store[j], 3 * PITERS * 16)
                pool.wait_ge(s_storeL[j], PITERS * 16)
            for n in range(NB):
                g = n // NG
                nc.gpsimd.indirect_dma_start(
                    out=final_rows[:, n, :], out_offset=None, in_=tables[3],
                    in_offset=bass.IndirectOffsetOnAxis(ap=ecol[:, 1, n:n + 1], axis=0)).then_inc(s_last[g], 16)
                nc.gpsimd.indirect_dma_start(
                    out=al[:, n, :], out_offset=None, in_=tableL,
                    in_offset=bass.IndirectOffsetOnAxis(ap=ecol[:, 0, n:n + 1], axis=0)).then_inc(s_last[g], 16)

        @block.scalar
        def _(act):
            act.sem_inc(s_hT, 1)
            act.sem_inc(s_quarter_out, 4)
            act.sem_inc(s_quarter_free, 4)
            act.wait_ge(s_in, 48)
            nc.scalar.copy(ident_b[:, :], ident).then_inc(s_constb, 1)
            nc.scalar.copy(tri_b[:, :], cst[:, C_TRI:C_TRI + P]).then_inc(s_constb, 1)

            def take_before(q):
                for b in range(NB):
                    act.wait_ge(s_before, q * NB + b + 1)
                    nc.scalar.copy(before[:, b, :], ps[:, 1, 0:ET]).then_inc(s_before_out, 1)

            def fill(q, h, i):
                t0 = i * (2 * SH) + h * SH
                cut = bass.ds(t0, SH) if not isinstance(i, int) else slice(t0, t0 + SH)
                nc.scalar.copy(rec_ring[:, h * SH:(h + 1) * SH, :], rec[q][:, cut, :])
                nc.scalar.copy(place_ring[:, h * SH:(h + 1) * SH], place[q][:, cut]).then_inc(s_recs, 1)

            def fill_scatter(q):
                act.wait_ge(s_place, q + 1)
                for h in range(2):
                    if q:
                        act.wait_ge(s_scat[h], q * SITERS * SH * 16)
                    fill(q, h, 0)
                with act.Fori(1, SITERS) as i:
                    for h in range(2):
                        hold(act, s_scat[h], i * (SH * 16) + q * SITERS * SH * 16, s_tok_act)
                        fill(q, h, i)

            def root(l):
                act.wait_ge(s_var, l + 1)
                nc.scalar.activation(rstd[:, :], mean_var[:, :, 1], ACT.Sqrt).then_inc(s_sd, 1)

            def project(l, start, end):
                c0 = l * NB

                def normalise(i, j):
                    hold(act, s_tr, i * NG + (c0 + j + 1), s_tok_act)
                    n = i * NG + j
                    nc.scalar.activation(h_ring[:, j, :].unsqueeze(1), X[:, bass.ds(n, 1), :], ACT.Relu,
                                         bias=shift[:, bass.ds(n, 1)], scale=rstd[:, bass.ds(n, 1)]).then_inc(s_h, 1)

                def take_transposed(i, j):
                    act.wait_ge(s_tr, i * NG + (c0 + j + 1 + NG))
                    if l == 0:
                        hold(act, s_quarter, i * (4 * NG) + (4 * j + 4), s_tok_act)
                    else:
                        hold(act, s_row, i * NG + (c0 - NB + j + 1), s_tok_act)
                    nc.scalar.copy(hT_ring[:, j, :, :].rearrange("p k n -> p (k n)"),
                                   ps[:, 2 + j % 2, 0:F]).then_inc(s_hT, 1)

                def take_quarters(i, j):
                    for q in range(4):
                        act.wait_ge(s_quarter, i * (4 * NG) + (4 * j + q + 1 + 4 * NG))
                        hold(act, s_quarter_free, i * (4 * NG) + (4 * j + q + 1), s_tok_act)
                        nc.scalar.copy(out_ring[:, q, :], ps[:, 4 + q, :]).then_inc(s_quarter_out, 1)

                with act.Fori(start, end) as i:
                    normalise(i, 0)
                    normalise(i, 1)
                    take_transposed(i, 0)
                    for j in range(NG):
                        if j + 2 < NG:
                            normalise(i, j + 2)
                        if j + 1 < NG:
                            take_transposed(i, j + 1)
                        if l == 0:
                            take_quarters(i, j)

            def copy_indices(l, q):
                act.wait_ge(s_slots[q], 16)
                with act.Fori(0, ITERS) as i:
                    for k in range(SETS):
                        hold(act, s_added, i * RING + (l * NT + (k + 1) * BLK), s_tok_act)
                        nc.scalar.copy(idx_ring[:, k * BLK:(k + 1) * BLK],
                                       slots[q][:, bass.ds(i * RING + k * BLK, BLK), 1 if l == 1 else 0]).then_inc(s_idx, 1)

            root(0)
            take_before(0)
            act.wait_ge(s_norm, 1)
            project(0, 0, 2)
            take_before(1)
            project(0, 2, PITERS)
            fill_scatter(0)
            copy_indices(0, 0)
            root(1)
            act.wait_ge(s_norm, 2)
            project(1, 0, PITERS)
            fill_scatter(1)
            act.wait_ge(s_negM, 1)
            nc.scalar.activation(logit, logit, ACT.Exp, bias=mx[:, 1:2]).then_inc(s_exp, 1)
            copy_indices(1, 0)
            root(2)
            act.wait_ge(s_norm, 3)
            project(2, 0, PITERS)
            copy_indices(2, 1)
            root(3)
            act.wait_ge(s_norm, 4)
            project(3, 0, PITERS)
            for g in range(PITERS):
                act.wait_ge(s_e3, g + 1)
                cut = slice(g * NG, (g + 1) * NG)
                nc.scalar.activation(sc2[:, cut, :], sc[:, cut, :], ACT.Exp).then_inc(s_e3x, 1)

        @block.vector
        def _(dve):
            done = [0]

            def step(ins):
                done[0] += 1
                ins.then_inc(s_prep, 1)
                dve.wait_ge(s_prep, done[0])

            V = nc.vector
            dve.sem_inc(s_added, RING)
            dve.sem_inc(s_row_out, NG)
            dve.sem_inc(s_row_free, NG)
            V.memset(ones_b[:, :], 1.0).then_inc(s_constb, 1)
            step(V.memset(ones_row[:, :], 1.0))
            step(V.memset(slots[0][:, :, :], 0.0))
            V.memset(slots[0][:, :, 2:3], -1.0).then_inc(s_blank, 1)

            def norm_stats(l):
                for n in range(NB):
                    last = V.bn_stats(stats[:, n, :], X[:, n, :])
                step(last)
                for n in range(NB):
                    last = V.bn_aggr(mean_var[:, n, :], stats[:, n, :])
                step(last)
                V.tensor_scalar_add(mean_var[:, :, 1], mean_var[:, :, 1], EPS).then_inc(s_var, 1)
                dve.wait_ge(s_sd, l + 1)
                step(V.reciprocal(rstd[:, :], rstd[:, :]))
                V.scalar_tensor_tensor(out=shift[:, :], in0=mean_var[:, :, 0], scalar=-1.0, in1=rstd[:, :],
                                       op0=ALU.mult, op1=ALU.mult).then_inc(s_norm, 1)

            def bucket(q):
                key, other = ecol[:, 1 - q, :], ecol[:, q, :]
                step(V.tensor_scalar(tmp_j[:, :], key, 7, None, ALU.arith_shift_right))
                step(V.tensor_copy(run[:, :], tmp_j[:, :]))
                V.tensor_tensor(member, run[:, :].unsqueeze(1).to_broadcast([P, NB, ET]),
                                iota[:, 0:NB].unsqueeze(2).to_broadcast([P, NB, ET]), ALU.is_equal).then_inc(s_member, 1)
                if q == 0:
                    step(V.scalar_tensor_tensor(out=rec[0][:, :, 0], in0=ecol[:, 0, :], scalar=float(R), in1=ecol[:, 2, :],
                                                op0=ALU.mult, op1=ALU.add))
                else:
                    step(V.tensor_copy(rec[q][:, :, 0], other))
                step(V.tensor_copy(rec[q][:, :, 1], ecol[:, 0, :]))
                step(V.tensor_copy(rec[q][:, :, 2], key))
                step(V.tensor_copy(rec[q][:, :, 3], wcol[:, :]))
                for b in range(NB):
                    dve.wait_ge(s_count, q * NB + b + 1)
                    V.tensor_copy(count[:, b, :], ps[:, 0, 0:ET]).then_inc(s_count_out, 1)
                dve.wait_ge(s_count_out, (q + 1) * NB)
                size, tiles, upto, first, start = (total[:, c, :] for c in range(5))
                step(V.reduce_sum(size, count, axis=AX.X))
                step(V.tensor_scalar_add(size, size, float(P - 1)))
                step(V.tensor_copy(total_i[:, :], size))
                step(V.tensor_scalar(total_i[:, :], total_i[:, :], 7, None, ALU.arith_shift_right))
                step(V.tensor_copy(tiles, total_i[:, :]))
                step(V.tensor_tensor_scan(upto, ones_row[:, 0:NB], tiles, 0.0, ALU.mult, ALU.add))
                step(V.tensor_sub(first, upto, tiles))
                step(V.tensor_scalar_mul(start, first, float(P)))
                step(V.memset(rank_f[:, :], 0.0))
                dve.wait_ge(s_before_out, (q + 1) * NB)
                for b in range(NB):
                    step(V.tensor_tensor_scan(run[:, :], ones_row[:, :], count[:, b, :], start[:, b:b + 1], ALU.mult, ALU.add))
                    step(V.tensor_add(run[:, :], run[:, :], before[:, b, :]))
                    step(V.tensor_mul(run[:, :], run[:, :], member[:, b, :]))
                    step(V.tensor_add(rank_f[:, :], rank_f[:, :], run[:, :]))
                step(V.tensor_copy(place[q][:, :], rank_f[:, :]))
                step(V.tensor_scalar(tmp_j[:, :], place[q][:, :], P - 1, None, ALU.bitwise_and))
                step(V.tensor_copy(run[:, :], tmp_j[:, :]))
                step(V.tensor_scalar(tmp_j[:, :], place[q][:, :], 7, None, ALU.arith_shift_right))
                step(V.scalar_tensor_tensor(out=rank_f[:, :], in0=run[:, :], scalar=float(NT), in1=tmp_j[:, :],
                                            op0=ALU.mult, op1=ALU.add))
                step(V.tensor_add(rank_f[:, ET - 1:ET], rank_f[:, ET - 1:ET], pad_row))
                V.tensor_copy(place[q][:, :], rank_f[:, :]).then_inc(s_place, 1)
                step(V.memset(tile_bucket[q][:, :], 0.0))
                for b in range(1, NB):
                    step(V.scalar_tensor_tensor(out=tile_bucket[q][:, :], in0=slot_no, scalar=first[:, b:b + 1],
                                                in1=tile_bucket[q][:, :], op0=ALU.is_ge, op1=ALU.add))
                step(V.tensor_copy(tile_bucket_i[q][:, :], tile_bucket[q][:, :]))

            def localise(q):
                dve.wait_ge(s_slots[q], 16)
                step(V.scalar_tensor_tensor(out=local[q][:, :], in0=tile_bucket[q][:, :], scalar=-float(P),
                                            in1=slots[q][:, :, 2], op0=ALU.mult, op1=ALU.add))

            def aggregate(l, q):
                width = F + H if l == 1 else F
                into = U if l == 1 else X
                with dve.Fori(0, ITERS) as i:
                    for k in range(SETS):
                        t0 = i * RING + k * BLK
                        blocks = i * SETS + (l * ITERS * SETS + k + 1)
                        tiles = i * RING + (l * NT + k * BLK)
                        buckets = [dve.value_load(tile_bucket_i[q][0:1, bass.ds(t0 + j, 1)], min_val=0, max_val=NB - 1)
                                   for j in range(BLK)]
                        V.tensor_tensor(onehot[:, k, :, :], iota.unsqueeze(1).to_broadcast([P, BLK, P]),
                                        local[q][:, bass.ds(t0, BLK)].unsqueeze(2).to_broadcast([P, BLK, P]),
                                        ALU.is_equal).then_inc(s_onehot, 1)
                        if l:
                            dve.wait_ge(s_rows[k], i * (BLK * 16) + (l * ITERS + 1) * BLK * 16)
                            cut = rows[:, k * BLK:(k + 1) * BLK, 0:F]
                            if l == 1:
                                weight = logit[:, bass.ds(t0, BLK), :]
                                V.tensor_tensor(cut.rearrange("p j (h c) -> p j h c", h=H),
                                                cut.rearrange("p j (h c) -> p j h c", h=H),
                                                weight.unsqueeze(3).to_broadcast([P, BLK, H, F // H]), ALU.mult)
                                V.tensor_scalar(rows[:, k * BLK:(k + 1) * BLK, F:F + H], weight, 1.0, None,
                                                ALU.mult).then_inc(s_scaled, 1)
                            else:
                                V.tensor_tensor(cut, cut, slots[q][:, bass.ds(t0, BLK), 3:4].to_broadcast([P, BLK, F]),
                                                ALU.mult).then_inc(s_scaled, 1)
                        for j in range(BLK):
                            dve.wait_ge(s_mm, tiles + (j + 1))
                            dve.wait_ge(s_added, tiles + (j + RING))
                            acc = into[:, bass.ds(buckets[j], 1), 0:width]
                            V.tensor_tensor(acc, acc, ps[:, j:j + 1, 0:width], ALU.add).then_inc(s_added, 1)
                dve.wait_ge(s_added, (l + 1) * NT + RING)

            def take_rows(l):
                with dve.Fori(0, PITERS) as i:
                    for j in range(NG):
                        c = i * NG + ((l - 1) * NB + j + 1)
                        dve.wait_ge(s_row, c + NG)
                        hold(dve, s_row_free, c, s_tok_dve)
                        bank = (4 + j) % 8
                        wide = FW if l == 3 else F
                        if l == 1:
                            V.tensor_copy(attn[:, bass.ds(i * NG + j, 1), :], ps[:, bank:bank + 1, F:FW]).then_inc(s_att, 1)
                        V.tensor_copy(row_ring[:, j, 0:wide], ps[:, bank, 0:wide]).then_inc(s_row_out, 1)

            def fold(W, A, order):
                for c, a in enumerate(order):
                    for k in range(KT):
                        step(V.tensor_tensor(folded, W[:, k, 0:F], A[:, a, :], ALU.mult))
                        step(V.reduce_sum(W[:, k, F + c * H:F + (c + 1) * H], folded.rearrange("p (h c) -> p h c", h=H),
                                          axis=AX.X))

            dve.wait_ge(s_in, 48)
            dve.wait_ge(s_x, 16)
            norm_stats(0)
            bucket(0)
            dve.wait_ge(s_w, 128)
            fold(W1, A1, (0, 1))
            fold(W3, A3, (1, 0))
            bucket(1)
            localise(0)
            dve.wait_ge(s_h, NB)
            step(V.tensor_add(X[:, :, :], X[:, :, :], bias0_b[:, :].unsqueeze(1).to_broadcast([P, NB, F])))
            aggregate(0, 0)

            norm_stats(1)
            take_rows(1)
            step(V.tensor_copy(tmp_i[:, :], slots[0][:, :, 1]))
            step(V.tensor_scalar(tmp_i[:, :], tmp_i[:, :], 7, None, ALU.arith_shift_right))
            step(V.tensor_copy(hi_f[:, 0, :], tmp_i[:, :]))
            step(V.scalar_tensor_tensor(out=lo_b[:, 0, :], in0=hi_f[:, 0, :], scalar=-float(P), in1=slots[0][:, :, 1],
                                        op0=ALU.mult, op1=ALU.add))
            step(V.tensor_copy(hi_f[:, 1, :], tile_bucket[0][:, :]))
            step(V.tensor_copy(lo_b[:, 1, :], local[0][:, :]))
            dve.wait_ge(s_att, NB)
            rest = attn_rest[:, :, :, :]
            step(V.tensor_copy(rest, attn[:, :, :].rearrange("p n (s h) -> p s n h", s=2)))
            for c in range(3):
                step(V.tensor_copy(attn_part[:, :, c, :, :], rest))
                step(V.tensor_sub(rest, rest, attn_part[:, :, c, :, :]))
            V.memset(U, 0.0).then_inc(s_pd, 1)
            with dve.Fori(0, NT // BLK) as i:
                t0 = i * BLK
                for s in range(2):
                    dve.wait_ge(s_bc, i * 2 + (s + 1))
                    V.tensor_scalar(onehotT[:, s, :], ps[:, 2 * s:2 * s + 2, :].rearrange("p b c -> p (b c)")[:, 0:BLK * P],
                                    part, None, ALU.is_equal).then_inc(s_ohT, 1)
                for s in range(2):
                    last = V.tensor_tensor(pick[:, :, s, :], iota[:, 0:NB].unsqueeze(1).to_broadcast([P, BLK, NB]),
                                           hi_f[:, s, bass.ds(t0, BLK)].unsqueeze(2).to_broadcast([P, BLK, NB]), ALU.is_equal)
                last.then_inc(s_chainl, 1)
                dve.wait_ge(s_chainl, i * 2 + 1)
                dve.wait_ge(s_picks, i + 1)
                grid = ps[:, 4:8, :].rearrange("p b (u c) -> p (b u) c", u=2)[:, 0:BLK, 0:2 * NB * H]
                V.tensor_tensor(picked[:, :, :].rearrange("p j (a h) -> p j a h", h=H),
                                grid.rearrange("p j (a h) -> p j a h", h=H),
                                pick[:, :, :, :].rearrange("p j s b -> p j (s b)").unsqueeze(3).to_broadcast([P, BLK, 2 * NB, H]),
                                ALU.mult).then_inc(s_chainl, 1)
                hold(dve, s_chainl, i * 2 + 2, s_tok_dve)
                V.reduce_sum(logit[:, bass.ds(t0, BLK), :], picked[:, :, :].rearrange("p j (a h) -> p j h a", h=H),
                             axis=AX.X).then_inc(s_pd, 1)
            dve.wait_ge(s_pd, NT // BLK + 1)
            step(V.scalar_tensor_tensor(out=logit, in0=logit, scalar=0.2, in1=logit, op0=ALU.mult, op1=ALU.max))
            step(V.tensor_tensor(logit, logit, slots[0][:, :, 3:4].to_broadcast([P, NT, H]), ALU.mult))
            step(V.tensor_scalar(off[:, :], slots[0][:, :, 2], 0.0, FAR, ALU.is_ge, ALU.mult))
            step(V.tensor_scalar_add(off[:, :], off[:, :], -FAR))
            step(V.tensor_tensor(logit, logit, off[:, :].unsqueeze(2).to_broadcast([P, NT, H]), ALU.add))
            V.reduce_max(mx[:, 0:1], logit.rearrange("p t h -> p (t h)"), axis=AX.X).then_inc(s_mx, 1)
            dve.wait_ge(s_mT, 1)
            step(V.reduce_max(mrow[0:1, 0:1], ps[0:1, 0, 0:P], axis=AX.X))
            V.tensor_scalar_mul(mrow[0:1, 1:2], mrow[0:1, 0:1], -1.0).then_inc(s_m1, 1)
            dve.wait_ge(s_mB, 1)
            V.tensor_copy(mx[:, 1:2], ps[:, 1, 0:1]).then_inc(s_negM, 1)
            dve.wait_ge(s_exp, 1)
            aggregate(1, 0)
            step(V.tensor_scalar_add(sc[:, :, :], U[:, :, F:F + H], 1e-10))
            step(V.reciprocal(sc[:, :, :], sc[:, :, :]))
            for h in range(H):
                cut = U[:, :, h * (F // H):(h + 1) * (F // H)]
                last = V.tensor_tensor(cut, cut, sc[:, :, h:h + 1].to_broadcast([P, NB, F // H]), ALU.mult)
            step(last)
            step(V.tensor_add(X[:, :, :], X[:, :, :], U[:, :, 0:F]))

            norm_stats(2)
            localise(1)
            take_rows(2)
            dve.wait_ge(s_h, 3 * NB)
            step(V.tensor_add(X[:, :, :], X[:, :, :], b2_b[:, :].unsqueeze(1).to_broadcast([P, NB, F])))
            aggregate(2, 1)

            norm_stats(3)
            take_rows(3)
            for g in range(PITERS):
                cut = slice(g * NG, (g + 1) * NG)
                s, e = sc[:, cut, :], sc2[:, cut, :]
                top, whole = sm[:, cut, 0], sm[:, cut, 1]
                dve.wait_ge(s_last[g], NG * 32)
                step(V.tensor_add(s, al[:, cut, :], final_rows[:, cut, F:F + H]))
                step(V.scalar_tensor_tensor(out=s, in0=s, scalar=0.01, in1=s, op0=ALU.mult, op1=ALU.max))
                step(V.reduce_max(top, s, axis=AX.X))
                V.tensor_tensor(s, s, sm[:, cut, 0:1].to_broadcast([P, NG, H]), ALU.subtract).then_inc(s_e3, 1)
                dve.wait_ge(s_e3x, g + 1)
                step(V.reduce_sum(whole, e, axis=AX.X))
                step(V.reciprocal(whole, whole))
                step(V.tensor_tensor(e, e, sm[:, cut, 1:2].to_broadcast([P, NG, H]), ALU.mult))
                for h in range(H):
                    r = final_rows[:, cut, h * (F // H):(h + 1) * (F // H)]
                    last = V.tensor_tensor(r, r, sc2[:, cut, h:h + 1].to_broadcast([P, NG, F // H]), ALU.mult)
                step(last)
                for h in range(1, H):
                    r = final_rows[:, cut, h * (F // H):(h + 1) * (F // H)]
                    step(V.tensor_add(final_rows[:, cut, 0:F // H], final_rows[:, cut, 0:F // H], r))
                for h in range(H):
                    xc = X[:, cut, h * (F // H):(h + 1) * (F // H)]
                    last = V.tensor_add(xc, xc, final_rows[:, cut, 0:F // H])
                last.then_inc(s_done, 1)

        @block.tensor
        def _(pe):
            mm = nc.tensor.matmul
            pe.sem_inc(s_tr, NG)
            pe.sem_inc(s_quarter, 4 * NG)
            pe.sem_inc(s_row, NG)

            def count_buckets(q):
                pe.wait_ge(s_member, q + 1)
                for b in range(NB):
                    if q or b:
                        pe.wait_ge(s_count_out, q * NB + b)
                    mm(ps[:, 0, 0:ET], ones_b[:, :], member[:, b, :], start=True, stop=True).then_inc(s_count, 1)
                    if q or b:
                        pe.wait_ge(s_before_out, q * NB + b)
                    mm(ps[:, 1, 0:ET], tri_b[:, :], member[:, b, :], start=True, stop=True).then_inc(s_before, 1)

            def project(l, start, end):
                c0 = l * NB
                W = (W0, W1, W2, W3)[l]
                wide = (2 * F, FW, F, FW)[l]

                def transpose(i, j):
                    pe.wait_ge(s_h, i * NG + (c0 + j + 1))
                    pe.wait_ge(s_hT, i * NG + (c0 + j + 1))
                    for k in range(KT):
                        last = nc.tensor.transpose(ps[:, 2 + j % 2, k * P:(k + 1) * P], h_ring[:, j, k * P:(k + 1) * P], ident)
                    last.then_inc(s_tr, 1)

                def products(i, j):
                    pe.wait_ge(s_hT, i * NG + (c0 + j + 2))
                    if l == 0:
                        for q in range(4):
                            pe.wait_ge(s_quarter_out, i * (4 * NG) + (4 * j + q + 1))
                            for k in range(KT):
                                last = mm(ps[:, 4 + q, :], hT_ring[:, j, k, :], W[:, k, q * wide:(q + 1) * wide],
                                          start=(k == 0), stop=(k == KT - 1))
                            last.then_inc(s_quarter, 1)
                    else:
                        bank = (4 + j) % 8
                        pe.wait_ge(s_row_out, i * NG + ((l - 1) * NB + j + 1))
                        for k in range(KT):
                            last = mm(ps[:, bank, 0:wide], hT_ring[:, j, k, :], W[:, k, :], start=(k == 0), stop=(k == KT - 1))
                        last.then_inc(s_row, 1)

                with pe.Fori(start, end) as i:
                    transpose(i, 0)
                    transpose(i, 1)
                    for j in range(NG):
                        products(i, j)
                        if j + 2 < NG:
                            transpose(i, j + 2)

            def aggregate(l):
                with pe.Fori(0, ITERS) as i:
                    for k in range(SETS):
                        blocks = i * SETS + (l * ITERS * SETS + k + 1)
                        tiles = i * RING + (l * NT + k * BLK)
                        pe.wait_ge(s_onehot, blocks)
                        if l == 0:
                            pe.wait_ge(s_rows[k], i * (BLK * 16) + BLK * 16)
                        else:
                            pe.wait_ge(s_scaled, i * SETS + ((l - 1) * ITERS * SETS + k + 1))
                        for j in range(BLK):
                            pe.wait_ge(s_added, tiles + (j + 1 - BLK + RING))
                            width = F + H if l == 1 else F
                            mm(ps[:, j, 0:width], onehot[:, k, j, :], rows[:, k * BLK + j, 0:width],
                               start=True, stop=True).then_inc(s_mm, 1)

            pe.wait_ge(s_constb, 3)
            count_buckets(0)
            pe.wait_ge(s_w, 128)
            project(0, 0, 2)
            count_buckets(1)
            project(0, 2, PITERS)
            aggregate(0)
            project(1, 0, PITERS)
            pe.wait_ge(s_pd, 1)
            with pe.Fori(0, NT // BLK) as i:
                t0 = i * BLK
                for s in range(2):
                    for j in range(BLK):
                        last = mm(ps[:, 2 * s + j // 4, (j % 4) * P:(j % 4 + 1) * P],
                                  lo_b[:, s, bass.ds(t0 + j, 1)].to_broadcast([P, P]), ident_b[:, :], start=True, stop=True)
                    last.then_inc(s_bc, 1)
                pe.wait_ge(s_ohT, i * 2 + 2)
                pe.wait_ge(s_pd, i + 1)
                for j in range(BLK):
                    for s in range(2):
                        at = (j % 2) * 256 + s * NB * H
                        for c in range(3):
                            last = mm(ps[:, 4 + j // 2, at:at + NB * H], onehotT[:, s, j * P:(j + 1) * P],
                                      attn_part[:, s, c, :, :].rearrange("p n h -> p (n h)"), start=(c == 0), stop=(c == 2))
                last.then_inc(s_picks, 1)
            pe.wait_ge(s_mx, 1)
            nc.tensor.transpose(ps[0:1, 0, 0:P], mx[:, 0:1], ident).then_inc(s_mT, 1)
            pe.wait_ge(s_m1, 1)
            mm(ps[:, 1, 0:1], ones_row[0:1, 0:P], mrow[0:1, 1:2], start=True, stop=True).then_inc(s_mB, 1)
            aggregate(1)
            project(2, 0, PITERS)
            aggregate(2)
            project(3, 0, PITERS)


_OUT = ((P, NB, F), "float32")


def kernel(**inputs):
    import numpy as np
    import concourse.bacc as bacc
    from concourse.bass_utils import run_bass_kernel_spmd as run

    def nodes(a):
        a = np.pad(np.asarray(a), ((0, NB * P - N), (0, 0)))
        return a.reshape(NB, P, F).transpose(1, 0, 2)

    def edges(a, fill):
        a = np.pad(np.asarray(a), (0, ET * P - E), constant_values=fill)
        return a.reshape(ET, P).T

    def deep(a):
        return np.asarray(a).reshape(KT, P, -1).transpose(1, 0, 2)

    consts = np.zeros((P, CW), np.float32)
    consts[:, C_IOTA:C_IOTA + P] = np.arange(P)
    consts[:, C_ID:C_ID + P] = np.eye(P)
    consts[:, C_TRI:C_TRI + P] = -(np.arange(P)[:, None] >= np.arange(P)[None, :]).astype(np.float32)
    consts[:, C_SLOT:C_SLOT + NT] = np.arange(NT)
    consts[:, C_PART] = np.arange(P)
    left = E - (ET - 1) * P
    consts[left:, C_PAD] = P * NT + np.arange(left, P)

    src, dst, kind = inputs["src"], inputs["dst"], inputs["edge_type_8"]
    arrays = {
        "x": nodes(inputs["x"]),
        "ecols": np.stack([edges(src, NB * P), edges(dst, NB * P), edges(kind, 0)], 1),
        "wcols": edges(inputs["edge_weight"], 0),
        "consts": consts,
        "w0": deep(np.asarray(inputs["L0_gnn_weight"]).transpose(2, 0, 1).reshape(F, R * F)),
        "bias0": np.asarray(inputs["L0_gnn_bias"]).reshape(1, F),
        "w1": deep(np.asarray(inputs["L1_gnn_W"]).transpose(1, 0, 2).reshape(F, F)),
        "a1": np.stack([np.asarray(inputs["L1_gnn_a_src"]).reshape(F), np.asarray(inputs["L1_gnn_a_dst"]).reshape(F)]),
        "w2": deep(inputs["L2_gnn_W"]),
        "b2": np.asarray(inputs["L2_gnn_b"]).reshape(1, F),
        "w3": deep(inputs["L3_gnn_weight"]),
        "a3": np.stack([np.asarray(inputs["L3_gnn_attn_l"]).reshape(F), np.asarray(inputs["L3_gnn_attn_r"]).reshape(F)]),
    }
    nc = bacc.Bacc("TRN2", target_bir_lowering=False, num_devices=1)
    maps, args = {}, []
    for name, a in arrays.items():
        a = np.ascontiguousarray(a)
        maps[f"in_{name}"] = a
        args.append(nc.dram_tensor(f"in_{name}", a.shape, mybir.dt.from_np(a.dtype), kind="ExternalInput").ap())
    o = nc.dram_tensor("out_0", _OUT[0], F32, kind="ExternalOutput").ap()
    build(nc, *args, o)
    r = run(nc, [maps], core_ids=[0])
    got = r.results[0]["out_0"]
    return np.ascontiguousarray(got.transpose(1, 0, 2).reshape(NB * P, F)[:N])
```

```python
from contextlib import ExitStack

import concourse.bass as bass
from concourse import mybir

F32 = mybir.dt.float32
BF16 = mybir.dt.bfloat16
I32 = mybir.dt.int32
ALU = mybir.AluOpType
ACT = mybir.ActivationFunctionType
AX = mybir.AxisListType

P = 128
N, F, E, R, H = 3125, 256, 53125, 8, 4
NB = -(-N // P)
ET = -(-E // P)
NT = ET + NB
BLK = 7
SETS = 3
RING = BLK * SETS
ITERS = NT // RING
assert NT == ITERS * RING
FW = F + 2 * H
RW = F + 8
SH = 8
SITERS = ET // (2 * SH)
assert ET == SITERS * 2 * SH
NG = 5
PITERS = NB // NG
KT = F // P
EPS = 1e-5
FAR = 1e30

C_IOTA, C_ID, C_TRI, C_SLOT, C_PART, C_PAD = 0, P, 2 * P, 3 * P, 3 * P + NT, 3 * P + NT + 1
C_MINUS = C_PAD + 1
CW = C_MINUS + 1
PAIRS = NT // BLK // 2
FIRST_SCATTER = 6
assert NT // BLK == 2 * PAIRS + 1


FETCH_FROM = NG + 1
FETCH = NT // (NB - FETCH_FROM)


def build(nc, x, ecols, wcols, erows, wrows, consts, w0, bias0, w1, a1, w2, b2, w3, a3, out):
    with ExitStack() as ctx:
        def sb(name, shape, dt=F32):
            return ctx.enter_context(nc.sbuf_tensor(name, shape, dt))

        def sem(name):
            return ctx.enter_context(nc.semaphore(name))

        def dram(name, shape, dt=F32):
            return nc.dram_tensor(name, shape, dt, kind="Internal").ap()

        table0_rows = dram("table0", [NB * P * R, F])
        table0 = table0_rows.rearrange("(n r) f -> n (r f)", r=R)
        tables = [None, dram("table1", [NB * P, F]), dram("table2", [NB * P, F]), dram("table3", [NB * P, FW])]
        tableL = dram("tableL", [NB * P, H])
        slot_rows = [dram("slots_dst", [P * NT + P, 4]), dram("slots_src", [P * NT + P, 4])]

        X = sb("X", [P, NB, F])
        cst = sb("cst", [P, CW])
        iota, ident = cst[:, C_IOTA:C_IOTA + P], cst[:, C_ID:C_ID + P]
        slot_no, part, pad_row = cst[:, C_SLOT:C_SLOT + NT], cst[:, C_PART:C_PART + 1], cst[:, C_PAD:C_PAD + 1]
        ident_b = sb("ident_b", [P, P], BF16)
        tri_b = sb("tri_b", [P, P], BF16)
        ones_b = sb("ones_b", [P, P], BF16)
        ones_row = sb("ones_row", [P, ET])
        bias0_b = sb("bias0_b", [P, F])
        b2_b = sb("b2_b", [P, F])
        W1 = sb("W1", [P, KT, FW])
        W2 = sb("W2", [P, KT, F])
        W3 = sb("W3", [P, KT, FW])

        edge_rows = dram("edge_rows", [NT * P, 4])

        ecol = sb("ecol", [P, 3, ET], I32)
        wcol = sb("wcol", [P, ET])
        rec_d = sb("rec_d", [P, NT, 4])
        rec_s = sb("rec_s", [P, ET, 4])
        rank_f = sb("rank_f", [P, ET])
        run = sb("run", [P, ET])
        tmp_i = sb("tmp_i", [P, NT], I32)
        tmp_j = sb("tmp_j", [P, ET], I32)
        place = [sb("place_dst", [P, ET], I32), sb("place_src", [P, ET], I32)]
        total = sb("total", [P, 2, 6, NB])
        total_i = sb("total_i", [P, NB], I32)
        tile_bucket = [sb("tile_bucket_d", [P, NT]), sb("tile_bucket_s", [P, NT])]
        tile_bucket_i = [sb("tile_bucket_di", [P, NT], I32), sb("tile_bucket_si", [P, NT], I32)]
        rec_ring = sb("rec_ring", [P, 2 * SH, 4])
        place_ring = sb("place_ring", [P, 2 * SH], I32)
        order_rec = sb("order_rec", [P, SH, 4])
        order_place = sb("order_place", [P, SH], I32)

        slots = [sb("slots_d", [P, NT, 4]), rec_d]
        local = [sb("local_d", [P, NT]), sb("local_s", [P, NT])]
        idx_ring = sb("idx_ring", [P, RING], I32)
        offset_i = sb("offset_i", [P, NT], I32)
        spread = sb("spread", [NB, 2, P])
        begun = sb("begun", [NB, NT])
        worst = sb("worst", [P, 2])
        unsorted_i = sb("unsorted_i", [P, 1], I32)

        arena = sb("arena", [P, 3 * NB * ET // 2])
        arena_b = arena[:, :].bitcast(BF16)
        member = arena_b[:, 0:NB * ET].rearrange("p (b t) -> p b t", b=NB)
        count = arena_b[:, NB * ET:2 * NB * ET].rearrange("p (b t) -> p b t", b=NB)
        before = arena_b[:, 2 * NB * ET:3 * NB * ET].rearrange("p (b t) -> p b t", b=NB)
        rows = arena[:, 0:RING * RW].rearrange("p (s f) -> p s f", s=RING)
        U = arena[:, RING * RW:RING * RW + NB * (F + H)].rearrange("p (n f) -> p n f", n=NB)
        final_rows = arena[:, 0:NB * FW].rearrange("p (n f) -> p n f", n=NB)
        oh_at = RING * RW + NB * (F + H)
        onehot = arena[:, oh_at:oh_at + RING * P].rearrange("p (k j c) -> p k j c", k=SETS, j=BLK)
        assert oh_at + RING * P <= 3 * NB * ET // 2

        W0 = sb("W0", [P, KT, R * F])
        w0_flat = W0[:, :, :].rearrange("p k c -> p (k c)")
        logit = w0_flat[:, 0:NT * H].rearrange("p (t h) -> p t h", h=H)
        h_ring = sb("h_ring", [P, NG, F])
        hT_ring = sb("hT_ring", [P, NG, KT, P])
        out_ring = sb("out_ring", [P, 4, 2 * F])
        row_ring = sb("row_ring", [P, NG, FW])
        A1, A3, folded = row_ring[:, 1:3, 0:F], row_ring[:, 3:5, 0:F], row_ring[:, 0, 0:F]
        stats = sb("stats", [P, NB, 6])
        mean_var = sb("mean_var", [P, NB, 2])
        rstd = sb("rstd", [P, NB])
        shift = sb("shift", [P, NB])

        attn = sb("attn", [P, NB, 2 * H])
        attn_rest = sb("attn_rest", [P, 2, NB, H])
        attn_part = sb("attn_part", [P, 2, 3, NB, H], BF16)
        lo_b = sb("lo_b", [P, 2, NT], BF16)
        hi_f = sb("hi_f", [P, 1, NT])
        onehotT_s = h_ring[:, :, :].rearrange("p j c -> p (j c)")[:, 0:BLK * P].bitcast(BF16).rearrange(
            "p (u c) -> p u c", u=2)
        onehotT_d = sb("onehotT_d", [P, 2, BLK * P], BF16)
        out_flat = out_ring[:, :, :].rearrange("p q c -> p (q c)")
        PK = NB + 1
        picked = out_flat[:, 0:BLK * PK * H].rearrange("p (j c) -> p j c", j=BLK)
        pick = out_flat[:, BLK * PK * H:BLK * PK * (H + 1)].rearrange("p (j b) -> p j b", j=BLK)
        distance = out_flat[:, BLK * PK * (H + 1):BLK * PK * (H + 1) + BLK * P // 2].bitcast(BF16)
        off = sb("off", [P, NT])
        row_src, row_kind = tmp_i[:, 0:ET], place[0][:, :]
        row_dst, row_next = local[0][:, 0:ET].bitcast(I32), local[1][:, 0:ET].bitcast(I32)
        row_w = off[:, 0:ET]
        row_rec = rec_d[:, 0:ET, :]
        mx = sb("mx", [P, 4])
        minus_part = cst[:, C_MINUS:C_MINUS + 1]
        mrow = sb("mrow", [1, 4])
        al = sb("al", [P, NB, H])
        sc = sb("sc", [P, NB, H])
        sc2 = sb("sc2", [P, NB, H])
        sm = sb("sm", [P, NB, 2])

        ps = ctx.enter_context(nc.psum_tensor("ps", [P, 8, 512], F32))

        s_cst = sem("s_cst")
        s_in = sem("s_in")
        s_x = sem("s_x")
        s_w = sem("s_w")
        s_prep = sem("s_prep")
        s_constb = sem("s_constb")
        s_member = sem("s_member")
        s_count = sem("s_count")
        s_before = sem("s_before")
        s_count_out = sem("s_count_out")
        s_before_out = sem("s_before_out")
        s_blank = sem("s_blank")
        s_blanked = sem("s_blanked")
        s_place = sem("s_place")
        s_recs = sem("s_recs")
        s_scat = [sem(f"s_scat{h}") for h in range(2)]
        s_slots = [sem("s_slots_d"), sem("s_slots_s")]
        s_local = sem("s_local")
        s_var = sem("s_var")
        s_sd = sem("s_sd")
        s_norm = sem("s_norm")
        s_h = sem("s_h")
        s_tr = sem("s_tr")
        s_hT = sem("s_hT")
        s_quarter = sem("s_quarter")
        s_quarter_out = sem("s_quarter_out")
        s_quarter_free = sem("s_quarter_free")
        s_store0 = [sem(f"s_store0_{q}") for q in range(4)]
        s_row = sem("s_row")
        s_row_out = sem("s_row_out")
        s_row_free = sem("s_row_free")
        s_store = [sem(f"s_store{j}") for j in range(NG)]
        s_storeL = [sem(f"s_storeL{j}") for j in range(NG)]
        s_idx = sem("s_idx")
        s_rows = [sem(f"s_rows{k}") for k in range(SETS)]
        s_onehot = sem("s_onehot")
        s_scaled = sem("s_scaled")
        s_mm = sem("s_mm")
        s_added = sem("s_added")
        s_att = sem("s_att")
        s_parts = sem("s_parts")
        s_bcast_src, s_bcast_dst = sem("s_bcast_src"), sem("s_bcast_dst")
        s_distance = sem("s_distance")
        s_onehot_src, s_onehot_dst = sem("s_onehot_src"), sem("s_onehot_dst")
        s_picked_mm = sem("s_picked_mm")
        s_pick = sem("s_pick")
        s_picked = sem("s_picked")
        s_edges = sem("s_edges")
        s_row_rec = sem("s_row_rec")
        s_worst = sem("s_worst")
        s_sorted = sem("s_sorted")
        s_order = sem("s_order")
        s_ordered = sem("s_ordered")
        s_dst_slots = sem("s_dst_slots")
        s_part, s_whole = sem("s_part"), sem("s_whole")
        s_sizes = sem("s_sizes")
        s_spread = sem("s_spread")
        s_begun = sem("s_begun")
        s_spread_out = sem("s_spread_out")
        s_offset = sem("s_offset")
        s_mx = sem("s_mx")
        s_mT = sem("s_mT")
        s_m1 = sem("s_m1")
        s_mB = sem("s_mB")
        s_negM = sem("s_negM")
        s_exp = sem("s_exp")
        s_last = [sem(f"s_last{g}") for g in range(PITERS)]
        s_e3 = sem("s_e3")
        s_e3x = sem("s_e3x")
        s_done = sem("s_done")
        s_out = sem("s_out")
        s_tok_act = sem("s_tok_act")
        s_tok_sp = sem("s_tok_sp")
        s_tok_pool = sem("s_tok_pool")
        s_tok_dve = sem("s_tok_dve")

        def hold(eng, s, value, token):
            eng.wait_ge(s, value)
            eng.sem_inc(token, 1)

        block = ctx.enter_context(nc.Block())

        @block.sync
        def _(sp):
            sp.dma_start(cst[:, :], consts).then_inc(s_cst, 16)
            sp.dma_start(X[:, :, :], x).then_inc(s_x, 16)
            sp.dma_start(ecol[:, :, :], ecols).then_inc(s_in, 16)
            sp.dma_start(wcol[:, :], wcols).then_inc(s_in, 16)
            for n, dst in enumerate((row_src, row_dst, row_next, row_kind)):
                sp.dma_start(dst, erows[:, n, :]).then_inc(s_in, 16)
            sp.dma_start(row_w, wrows).then_inc(s_in, 16)
            sp.dma_start(W0[:, :, :], w0).then_inc(s_w, 16)
            for dst, src in ((W1[:, :, 0:F], w1), (W2[:, :, :], w2), (W3[:, :, 0:F], w3)):
                sp.dma_start(dst, src).then_inc(s_w, 16)
            for dst, src in ((A1, a1), (A3, a3)):
                sp.dma_start(dst, src.unsqueeze(0).to_broadcast([P, 2, F])).then_inc(s_w, 16)
            for dst, src in ((bias0_b, bias0), (b2_b, b2)):
                sp.dma_start(dst[:, :], src.to_broadcast([P, F])).then_inc(s_w, 16)
            sp.wait_ge(s_blank, 1)
            for q in range(2):
                sp.dma_start(slot_rows[q][0:P * NT, :].rearrange("(p t) c -> p (t c)", p=P),
                             slots[0][:, :, :].rearrange("p t c -> p (t c)")).then_inc(s_blanked, 16)
            sp.dma_start(edge_rows[ET * P:NT * P, :].rearrange("(p t) c -> p (t c)", p=P),
                         slots[0][:, 0:NB, :].rearrange("p t c -> p (t c)")).then_inc(s_edges, 16)
            sp.wait_ge(s_row_rec, 1)
            sp.dma_start(edge_rows[0:ET * P, :].rearrange("(p t) c -> p (t c)", p=P),
                         row_rec.rearrange("p t c -> p (t c)")).then_inc(s_edges, 16)

            def load_slots(q):
                for h in range(2):
                    sp.wait_ge(s_scat[h], SITERS * SH * 16)
                sp.dma_start(slots[q][:, :, :].rearrange("p t c -> p (t c)"),
                             slot_rows[q][0:P * NT, :].rearrange("(p t) c -> p (t c)", p=P)).then_inc(s_slots[q], 16)

            for q in range(4):
                sp.wait_ge(s_quarter_out, 4 + q + 1)
                sp.dma_start(table0[0:P, q * 2 * F:(q + 1) * 2 * F], out_ring[:, q, :]).then_inc(s_store0[q], 16)

            def store_quarters(n):
                for q in range(4):
                    sp.wait_ge(s_store0[q], n * 16)
                    sp.sem_inc(s_quarter_free, 1)
                    hold(sp, s_quarter_out, n * 4 + (4 + q + 1), s_tok_sp)
                    sp.dma_start(table0[bass.ds(n * P, P), q * 2 * F:(q + 1) * 2 * F],
                                 out_ring[:, q, :]).then_inc(s_store0[q], 16)

            def fetch_slots(t0, tiles):
                _, firsts = nc.values_load_multi_w_load_instructions(
                    offset_i[0:1, bass.ds(t0, tiles)], engines=[mybir.EngineType.SP], min_val=0, max_val=(NT - 1) * P,
                    skip_runtime_bounds_check_because="128 times the tile's number, less gaps that it is past")
                for j in range(tiles):
                    sp.dma_start(slots[0][:, bass.ds(t0 + j, 1), :].rearrange("p t c -> p (t c)"),
                                 edge_rows[bass.ds(firsts[j], P), :]).then_inc(s_slots[0], 16)

            with sp.Fori(1, FETCH_FROM) as n:
                store_quarters(n)
            sp.wait_ge(s_edges, 32)
            sp.wait_ge(s_blanked, 32)
            sp.wait_ge(s_offset, 1)
            sp.sem_inc(s_tok_sp, 1)
            with sp.Fori(FETCH_FROM, NB) as n:
                store_quarters(n)
                fetch_slots(n * FETCH - FETCH_FROM * FETCH, FETCH)
            fetch_slots((NB - FETCH_FROM) * FETCH, NT - (NB - FETCH_FROM) * FETCH)

            def store_rows(l):
                def turn(i, first):
                    for j in range(NG):
                        if not (first and l == 1):
                            hold(sp, s_store[j], (i + (l - 1) * PITERS) * 16, s_tok_sp)
                            if l == 3 and not first:
                                hold(sp, s_storeL[j], i * 16, s_tok_sp)
                            sp.sem_inc(s_row_free, 1)
                        hold(sp, s_row_out, (i + (l - 1) * PITERS) * NG + (j + 1 + NG), s_tok_sp)
                        at = i * (NG * P) + j * P
                        wide = FW if l == 3 else F
                        sp.dma_start(tables[l][bass.ds(at, P), :] if not first else tables[l][j * P:(j + 1) * P, :],
                                     row_ring[:, j, 0:wide]).then_inc(s_store[j], 16)
                        if l == 3:
                            sp.dma_start(tableL[bass.ds(at, P), :] if not first else tableL[j * P:(j + 1) * P, :],
                                         row_ring[:, j, F + H:FW]).then_inc(s_storeL[j], 16)
                turn(0, True)
                with sp.Fori(1, PITERS) as i:
                    turn(i, False)

            store_rows(1)
            load_slots(1)
            store_rows(2)
            store_rows(3)
            for g in range(PITERS):
                sp.wait_ge(s_done, g + 1)
                sp.dma_start(out[:, g * NG:(g + 1) * NG, :], X[:, g * NG:(g + 1) * NG, :]).then_inc(s_out, 16)
            sp.wait_ge(s_out, PITERS * 16)

        @block.gpsimd
        def _(pool):
            def scatter_half(i, h):
                cut = bass.ds(i * (2 * SH) + h * SH, SH)
                nc.gpsimd.tensor_copy(rec_ring[:, h * SH:(h + 1) * SH, :], rec_s[:, cut, :]).then_inc(s_recs, 1)
                nc.gpsimd.tensor_copy(place_ring[:, h * SH:(h + 1) * SH], place[1][:, cut]).then_inc(s_recs, 1)
                hold(pool, s_recs, i * 4 + (2 * h + 2), s_tok_pool)
                for j in range(h * SH, (h + 1) * SH):
                    nc.gpsimd.indirect_dma_start(
                        out=slot_rows[1], out_offset=bass.IndirectOffsetOnAxis(ap=place_ring[:, j:j + 1], axis=0),
                        in_=rec_ring[:, j, :], in_offset=None).then_inc(s_scat[h], 16)

            def scatter(start, end):
                with pool.Fori(start, end) as i:
                    for h in range(2):
                        hold(pool, s_scat[h], i * (SH * 16), s_tok_pool)
                        scatter_half(i, h)

            def order_dst():
                pool.wait_ge(s_place, 2)
                t = nc.gpsimd.tensor_copy(rec_d[:, 0:ET, 0], ecol[:, 0, :])
                t.then_inc(s_order, 1)
                pool.wait_ge(s_order, 1)
                nc.gpsimd.tensor_scalar(rec_d[:, 0:ET, 0], rec_d[:, 0:ET, 0], float(R), None, ALU.mult).then_inc(s_order, 1)
                nc.gpsimd.tensor_copy(rec_d[:, 0:ET, 1], ecol[:, 2, :]).then_inc(s_order, 1)
                pool.wait_ge(s_order, 3)
                nc.gpsimd.tensor_tensor(rec_d[:, 0:ET, 0], rec_d[:, 0:ET, 0], rec_d[:, 0:ET, 1], ALU.add).then_inc(s_order, 1)
                pool.wait_ge(s_order, 4)
                nc.gpsimd.tensor_copy(rec_d[:, 0:ET, 1], ecol[:, 0, :]).then_inc(s_order, 1)
                nc.gpsimd.tensor_copy(rec_d[:, 0:ET, 2], ecol[:, 1, :]).then_inc(s_order, 1)
                nc.gpsimd.tensor_copy(rec_d[:, 0:ET, 3], wcol[:, :]).then_inc(s_order, 1)
                pool.wait_ge(s_order, 7)
                with pool.Fori(0, ET // SH) as i:
                    nc.gpsimd.tensor_copy(order_rec[:, :, :], rec_d[:, bass.ds(i * SH, SH), :]).then_inc(s_order, 1)
                    nc.gpsimd.tensor_copy(order_place[:, :], place[0][:, bass.ds(i * SH, SH)]).then_inc(s_order, 1)
                    hold(pool, s_order, i * 2 + 9, s_tok_pool)
                    for j in range(SH):
                        nc.gpsimd.indirect_dma_start(
                            out=slot_rows[0], out_offset=bass.IndirectOffsetOnAxis(ap=order_place[:, j:j + 1], axis=0),
                            in_=order_rec[:, j, :], in_offset=None).then_inc(s_ordered, 16)
                    hold(pool, s_ordered, i * (SH * 16) + SH * 16, s_tok_pool)
                pool.dma_start(slots[0][:, :, :].rearrange("p t c -> p (t c)"),
                               slot_rows[0][0:P * NT, :].rearrange("(p t) c -> p (t c)", p=P)).then_inc(s_ordered, 16)
                pool.wait_ge(s_ordered, (ET + 1) * 16)

            def gather(l, table):
                with pool.Fori(0, ITERS) as i:
                    for k in range(SETS):
                        hold(pool, s_idx, i * SETS + (l * ITERS * SETS + k + 1), s_tok_pool)
                        for j in range(k * BLK, (k + 1) * BLK):
                            nc.gpsimd.indirect_dma_start(
                                out=rows[:, j, 0:F], out_offset=None, in_=table,
                                in_offset=bass.IndirectOffsetOnAxis(ap=idx_ring[:, j:j + 1], axis=0)).then_inc(s_rows[k], 16)

            pool.wait_ge(s_worst, 1)
            nc.gpsimd.partition_all_reduce(worst[:, 1:2], worst[:, 0:1], P, bass.bass_isa.ReduceOp.max).then_inc(s_sorted, 1)
            pool.wait_ge(s_sorted, 1)
            nc.gpsimd.tensor_scalar(unsorted_i[:, :], worst[:, 1:2], 0.0, None, ALU.is_gt).then_inc(s_sorted, 1)
            pool.wait_ge(s_sorted, 2)
            pool.sem_inc(s_tok_pool, 1)
            is_unsorted = pool.value_load(unsorted_i[0:1, 0:1], min_val=0, max_val=1)
            pool.wait_ge(s_blanked, 32)
            pool.wait_ge(s_place, 1)
            pool.sem_inc(s_tok_pool, 1)
            scatter_half(0, 0)
            scatter_half(0, 1)
            scatter(1, FIRST_SCATTER)
            pool.wait_ge(s_slots[0], NT * 16)
            pool.wait_ge(s_edges, 32)
            pool.sem_inc(s_tok_pool, 1)
            with pool.If(is_unsorted):
                order_dst()
            pool.sem_inc(s_dst_slots, 1)
            for q in range(4):
                pool.wait_ge(s_store0[q], NB * 16)
            pool.wait_ge(s_place, 2)
            pool.sem_inc(s_tok_pool, 1)
            gather(0, table0_rows)
            scatter(FIRST_SCATTER, SITERS)
            for l in (1, 2):
                for j in range(NG):
                    pool.wait_ge(s_store[j], l * PITERS * 16)
                gather(l, tables[l])
            for j in range(NG):
                pool.wait_ge(s_store[j], 3 * PITERS * 16)
                pool.wait_ge(s_storeL[j], PITERS * 16)
            for n in range(NB):
                g = n // NG
                nc.gpsimd.indirect_dma_start(
                    out=final_rows[:, n, :], out_offset=None, in_=tables[3],
                    in_offset=bass.IndirectOffsetOnAxis(ap=ecol[:, 1, n:n + 1], axis=0)).then_inc(s_last[g], 16)
                nc.gpsimd.indirect_dma_start(
                    out=al[:, n, :], out_offset=None, in_=tableL,
                    in_offset=bass.IndirectOffsetOnAxis(ap=ecol[:, 0, n:n + 1], axis=0)).then_inc(s_last[g], 16)

        @block.scalar
        def _(act):
            act.sem_inc(s_hT, 1)
            act.sem_inc(s_quarter_out, 4)
            act.sem_inc(s_quarter_free, 4)
            act.sem_inc(s_onehot_src, 1)
            act.wait_ge(s_cst, 16)
            nc.scalar.copy(ident_b[:, :], ident).then_inc(s_constb, 1)
            nc.scalar.copy(tri_b[:, :], cst[:, C_TRI:C_TRI + P]).then_inc(s_constb, 1)

            def take_before(q):
                for b in range(NB):
                    act.wait_ge(s_before, q * NB + b + 1)
                    nc.scalar.copy(before[:, b, :], ps[:, 1, 0:ET]).then_inc(s_before_out, 1)

            def root(l):
                act.wait_ge(s_var, l + 1)
                nc.scalar.activation(rstd[:, :], mean_var[:, :, 1], ACT.Sqrt).then_inc(s_sd, 1)

            def project(l, start, end):
                c0 = l * NB

                def normalise(i, j):
                    hold(act, s_tr, i * NG + (c0 + j + 1), s_tok_act)
                    n = i * NG + j
                    nc.scalar.activation(h_ring[:, j, :].unsqueeze(1), X[:, bass.ds(n, 1), :], ACT.Relu,
                                         bias=shift[:, bass.ds(n, 1)], scale=rstd[:, bass.ds(n, 1)]).then_inc(s_h, 1)

                def take_transposed(i, j):
                    act.wait_ge(s_tr, i * NG + (c0 + j + 1 + NG))
                    if l == 0:
                        hold(act, s_quarter, i * (4 * NG) + (4 * j + 4), s_tok_act)
                    else:
                        hold(act, s_row, i * NG + (c0 - NB + j + 1), s_tok_act)
                    nc.scalar.copy(hT_ring[:, j, :, :].rearrange("p k n -> p (k n)"),
                                   ps[:, 2 + j % 2, 0:F]).then_inc(s_hT, 1)

                def take_quarters(i, j):
                    for q in range(4):
                        act.wait_ge(s_quarter, i * (4 * NG) + (4 * j + q + 1 + 4 * NG))
                        hold(act, s_quarter_free, i * (4 * NG) + (4 * j + q + 1), s_tok_act)
                        nc.scalar.copy(out_ring[:, q, :], ps[:, 4 + q, :]).then_inc(s_quarter_out, 1)

                with act.Fori(start, end) as i:
                    normalise(i, 0)
                    normalise(i, 1)
                    take_transposed(i, 0)
                    for j in range(NG):
                        if j + 2 < NG:
                            normalise(i, j + 2)
                        if j + 1 < NG:
                            take_transposed(i, j + 1)
                        if l == 0:
                            take_quarters(i, j)

            def copy_indices(l, q):
                if q == 0:
                    act.wait_ge(s_dst_slots, 1)
                else:
                    act.wait_ge(s_slots[1], 16)
                with act.Fori(0, ITERS) as i:
                    for k in range(SETS):
                        hold(act, s_added, i * RING + (l * NT + (k + 1) * BLK), s_tok_act)
                        nc.scalar.copy(idx_ring[:, k * BLK:(k + 1) * BLK],
                                       slots[q][:, bass.ds(i * RING + k * BLK, BLK), 1 if l == 1 else 0]).then_inc(s_idx, 1)

            root(0)
            act.wait_ge(s_norm, 1)
            project(0, 0, 1)
            take_before(0)
            project(0, 1, 4)
            take_before(1)
            project(0, 4, PITERS)
            copy_indices(0, 0)
            root(1)
            act.wait_ge(s_norm, 2)
            project(1, 0, PITERS)

            def source_onehot(count, u):
                hold(act, s_onehot_src, count + 1, s_tok_act)
                act.wait_ge(s_bcast_src, count + 1)
                nc.scalar.activation(distance, ps[:, 0:2, :].rearrange("p b c -> p (b c)")[:, 0:BLK * P], ACT.Abs,
                                     bias=minus_part).then_inc(s_distance, 1)
                act.wait_ge(s_distance, count + 2)
                hold(act, s_picked_mm, count + 1, s_tok_act)
                nc.scalar.activation(onehotT_s[:, u, :], distance, ACT.Relu, bias=1.0, scale=-1.0).then_inc(s_onehot_src, 1)

            act.wait_ge(s_att, NB)
            source_onehot(0, 0)
            with act.Fori(0, PAIRS) as i:
                source_onehot(i * 2 + 1, 1)
                source_onehot(i * 2 + 2, 0)
            act.wait_ge(s_negM, 1)
            nc.scalar.activation(logit, logit, ACT.Exp, bias=mx[:, 1:2]).then_inc(s_exp, 1)
            copy_indices(1, 0)
            root(2)
            act.wait_ge(s_norm, 3)
            project(2, 0, PITERS)
            copy_indices(2, 1)
            root(3)
            act.wait_ge(s_norm, 4)
            project(3, 0, PITERS)
            for g in range(PITERS):
                act.wait_ge(s_e3, g + 1)
                cut = slice(g * NG, (g + 1) * NG)
                nc.scalar.activation(sc2[:, cut, :], sc[:, cut, :], ACT.Exp).then_inc(s_e3x, 1)

        @block.vector
        def _(dve):
            done = [0]

            def step(ins):
                done[0] += 1
                ins.then_inc(s_prep, 1)
                dve.wait_ge(s_prep, done[0])

            V = nc.vector
            dve.sem_inc(s_added, RING)
            dve.sem_inc(s_row_out, NG)
            dve.sem_inc(s_row_free, NG)
            dve.sem_inc(s_picked, 2)
            V.memset(ones_b[:, :], 1.0).then_inc(s_constb, 1)
            step(V.memset(ones_row[:, :], 1.0))
            step(V.memset(slots[0][:, :, :], 0.0))
            V.memset(slots[0][:, :, 2:3], -1.0).then_inc(s_blank, 1)

            def norm_stats(l):
                for n in range(NB):
                    last = V.bn_stats(stats[:, n, :], X[:, n, :])
                step(last)
                for n in range(NB):
                    last = V.bn_aggr(mean_var[:, n, :], stats[:, n, :])
                step(last)
                V.tensor_scalar_add(mean_var[:, :, 1], mean_var[:, :, 1], EPS).then_inc(s_var, 1)
                dve.wait_ge(s_sd, l + 1)
                step(V.reciprocal(rstd[:, :], rstd[:, :]))
                V.scalar_tensor_tensor(out=shift[:, :], in0=mean_var[:, :, 0], scalar=-1.0, in1=rstd[:, :],
                                       op0=ALU.mult, op1=ALU.mult).then_inc(s_norm, 1)

            def mark_members(q):
                step(V.tensor_scalar(tmp_j[:, :], ecol[:, 1 - q, :], 7, None, ALU.arith_shift_right))
                step(V.tensor_copy(run[:, :], tmp_j[:, :]))
                return V.tensor_tensor(member, run[:, :].unsqueeze(1).to_broadcast([P, NB, ET]),
                                       iota[:, 0:NB].unsqueeze(2).to_broadcast([P, NB, ET]), ALU.is_equal)

            def take_counts(c):
                for b in range(NB):
                    dve.wait_ge(s_count, c * NB + b + 1)
                    V.tensor_copy(count[:, b, :], ps[:, 0, 0:ET]).then_inc(s_count_out, 1)
                dve.wait_ge(s_count_out, (c + 1) * NB)

            def place_buckets(q):
                size, tiles, upto, first, start, gap = (total[:, q, c, :] for c in range(6))
                step(V.tensor_scalar_add(start, size, float(P - 1)))
                step(V.tensor_copy(total_i[:, :], start))
                step(V.tensor_scalar(total_i[:, :], total_i[:, :], 7, None, ALU.arith_shift_right))
                step(V.tensor_copy(tiles, total_i[:, :]))
                step(V.tensor_tensor_scan(upto, ones_row[:, 0:NB], tiles, 0.0, ALU.mult, ALU.add))
                step(V.tensor_sub(first, upto, tiles))
                step(V.tensor_scalar_mul(start, first, float(P)))
                step(V.memset(gap[:, 0:1], 0.0))
                V.scalar_tensor_tensor(out=gap[:, 1:NB], in0=tiles[:, 0:NB - 1], scalar=float(P), in1=size[:, 0:NB - 1],
                                       op0=ALU.mult, op1=ALU.subtract).then_inc(s_sizes, 1)

            def spread_buckets(q):
                dve.wait_ge(s_spread, 2 * q + 1)
                step(V.tensor_copy(spread[:, :, :], ps[0:NB, 0, 0:2 * P].rearrange("b (c m) -> b c m", c=2)))
                V.tensor_scalar(begun[:, :], slot_no[0:NB, :], spread[:, 0, 0:1], None, ALU.is_ge).then_inc(s_begun, 1)
                dve.wait_ge(s_spread, 2 * q + 2)
                step(V.tensor_scalar_add(tile_bucket[q][:, :], ps[:, 0, 0:NT], -1.0))
                V.tensor_copy(tile_bucket_i[q][:, :], tile_bucket[q][:, :]).then_inc(s_spread_out, 1)
                if q == 0:
                    V.scalar_tensor_tensor(out=offset_i[:, :], in0=slot_no, scalar=float(P), in1=ps[:, 1, 0:NT],
                                           op0=ALU.mult, op1=ALU.subtract).then_inc(s_offset, 1)

            def rank_edges(q):
                start = total[:, q, 4, :]
                step(V.memset(rank_f[:, :], 0.0))
                dve.wait_ge(s_before_out, (2 - q) * NB)
                for b in range(NB):
                    step(V.tensor_tensor_scan(run[:, :], ones_row[:, :], count[:, b, :], start[:, b:b + 1], ALU.mult, ALU.add))
                    step(V.tensor_add(run[:, :], run[:, :], before[:, b, :]))
                    step(V.tensor_mul(run[:, :], run[:, :], member[:, b, :]))
                    step(V.tensor_add(rank_f[:, :], rank_f[:, :], run[:, :]))
                step(V.tensor_copy(place[q][:, :], rank_f[:, :]))
                step(V.tensor_scalar(tmp_j[:, :], place[q][:, :], P - 1, None, ALU.bitwise_and))
                step(V.tensor_copy(run[:, :], tmp_j[:, :]))
                step(V.tensor_scalar(tmp_j[:, :], place[q][:, :], 7, None, ALU.arith_shift_right))
                step(V.scalar_tensor_tensor(out=rank_f[:, :], in0=run[:, :], scalar=float(NT), in1=tmp_j[:, :],
                                            op0=ALU.mult, op1=ALU.add))
                step(V.tensor_add(rank_f[:, ET - 1:ET], rank_f[:, ET - 1:ET], pad_row))
                V.tensor_copy(place[q][:, :], rank_f[:, :]).then_inc(s_place, 1)

            def localise(q):
                dve.wait_ge(s_slots[1] if q else s_dst_slots, 16 if q else 1)
                step(V.scalar_tensor_tensor(out=local[q][:, :], in0=tile_bucket[q][:, :], scalar=-float(P),
                                            in1=slots[q][:, :, 2], op0=ALU.mult, op1=ALU.add))

            def aggregate(l, q):
                width = F + H if l == 1 else F
                into = U if l == 1 else X

                def prepare(i, k):
                    t0 = i * RING + k * BLK
                    V.tensor_tensor(onehot[:, k, :, :], iota.unsqueeze(1).to_broadcast([P, BLK, P]),
                                    local[q][:, bass.ds(t0, BLK)].unsqueeze(2).to_broadcast([P, BLK, P]),
                                    ALU.is_equal).then_inc(s_onehot, 1)
                    if l == 0:
                        return
                    dve.wait_ge(s_rows[k], i * (BLK * 16) + (l * ITERS + 1) * BLK * 16)
                    cut = rows[:, k * BLK:(k + 1) * BLK, 0:F]
                    if l == 1:
                        weight = logit[:, bass.ds(t0, BLK), :]
                        V.tensor_tensor(cut.rearrange("p j (h c) -> p j h c", h=H),
                                        cut.rearrange("p j (h c) -> p j h c", h=H),
                                        weight.unsqueeze(3).to_broadcast([P, BLK, H, F // H]), ALU.mult)
                        V.tensor_scalar(rows[:, k * BLK:(k + 1) * BLK, F:F + H], weight, 1.0, None,
                                        ALU.mult).then_inc(s_scaled, 1)
                    else:
                        V.tensor_tensor(cut, cut, slots[q][:, bass.ds(t0, BLK), 3:4].to_broadcast([P, BLK, F]),
                                        ALU.mult).then_inc(s_scaled, 1)

                def add_up(i, k):
                    tiles = i * RING + (l * NT + k * BLK)
                    _, buckets = nc.values_load_multi_w_load_instructions(
                        tile_bucket_i[q][0:1, bass.ds(i * RING + k * BLK, BLK)], engines=[mybir.EngineType.DVE],
                        min_val=0, max_val=NB - 1,
                        skip_runtime_bounds_check_because="a count of bucket starts less one, at most NB - 1")
                    for j in range(BLK):
                        dve.wait_ge(s_mm, tiles + (j + 1))
                        dve.wait_ge(s_added, tiles + (j + RING))
                        acc = into[:, bass.ds(buckets[j], 1), 0:width]
                        V.tensor_tensor(acc, acc, ps[:, j:j + 1, 0:width], ALU.add).then_inc(s_added, 1)

                prepare(0, 0)
                with dve.Fori(0, ITERS - 1) as i:
                    for k in range(SETS):
                        prepare(i + (k + 1) // SETS, (k + 1) % SETS)
                        add_up(i, k)
                for k in range(SETS):
                    if k + 1 < SETS:
                        prepare(ITERS - 1, k + 1)
                    add_up(ITERS - 1, k)
                dve.wait_ge(s_added, (l + 1) * NT + RING)

            def take_rows(l):
                with dve.Fori(0, PITERS) as i:
                    for j in range(NG):
                        c = i * NG + ((l - 1) * NB + j + 1)
                        dve.wait_ge(s_row, c + NG)
                        hold(dve, s_row_free, c, s_tok_dve)
                        bank = (4 + j) % 8
                        wide = FW if l == 3 else F
                        if l == 1:
                            V.tensor_copy(attn[:, bass.ds(i * NG + j, 1), :], ps[:, bank:bank + 1, F:FW]).then_inc(s_att, 1)
                        V.tensor_copy(row_ring[:, j, 0:wide], ps[:, bank, 0:wide]).then_inc(s_row_out, 1)

            def fold(W, A, order):
                for c, a in enumerate(order):
                    for k in range(KT):
                        step(V.tensor_tensor(folded, W[:, k, 0:F], A[:, a, :], ALU.mult))
                        step(V.reduce_sum(W[:, k, F + c * H:F + (c + 1) * H], folded.rearrange("p (h c) -> p h c", h=H),
                                          axis=AX.X))

            dve.wait_ge(s_x, 16)
            norm_stats(0)
            dve.wait_ge(s_cst, 16)
            dve.wait_ge(s_in, 7 * 16)
            step(V.tensor_tensor(run[:, :], row_dst, row_next, ALU.subtract))
            V.reduce_max(worst[:, 0:1], run[:, :], axis=AX.X).then_inc(s_worst, 1)
            step(V.scalar_tensor_tensor(out=row_rec[:, :, 0], in0=row_src, scalar=float(R), in1=row_kind,
                                        op0=ALU.mult, op1=ALU.add))
            step(V.tensor_copy(row_rec[:, :, 1], row_src))
            step(V.tensor_copy(row_rec[:, :, 2], row_dst))
            V.tensor_copy(row_rec[:, :, 3], row_w).then_inc(s_row_rec, 1)
            step(mark_members(0))
            V.reduce_sum(total[:, 0, 1, :], member, axis=AX.X).then_inc(s_part, 1)
            dve.wait_ge(s_whole, 1)
            step(V.tensor_copy(total[:, 0, 0, :], ps[:, 0, 0:NB]))
            place_buckets(0)
            spread_buckets(0)
            mark_members(1).then_inc(s_member, 1)
            step(V.tensor_copy(rec_s[:, :, 0], ecol[:, 1, :]))
            step(V.memset(rec_s[:, :, 1], 0.0))
            step(V.tensor_copy(rec_s[:, :, 2], ecol[:, 0, :]))
            step(V.tensor_copy(rec_s[:, :, 3], wcol[:, :]))
            take_counts(0)
            step(V.reduce_sum(total[:, 1, 0, :], count, axis=AX.X))
            place_buckets(1)
            rank_edges(1)
            spread_buckets(1)
            mark_members(0).then_inc(s_member, 1)
            take_counts(1)
            rank_edges(0)
            dve.wait_ge(s_w, 128)
            fold(W1, A1, (0, 1))
            fold(W3, A3, (1, 0))
            localise(0)
            dve.wait_ge(s_h, NB)
            step(V.tensor_add(X[:, :, :], X[:, :, :], bias0_b[:, :].unsqueeze(1).to_broadcast([P, NB, F])))
            aggregate(0, 0)

            norm_stats(1)
            take_rows(1)
            step(V.tensor_copy(tmp_i[:, :], slots[0][:, :, 1]))
            step(V.tensor_scalar(tmp_i[:, :], tmp_i[:, :], 7, None, ALU.arith_shift_right))
            step(V.tensor_copy(hi_f[:, 0, :], tmp_i[:, :]))
            step(V.scalar_tensor_tensor(out=lo_b[:, 0, :], in0=hi_f[:, 0, :], scalar=-float(P), in1=slots[0][:, :, 1],
                                        op0=ALU.mult, op1=ALU.add))
            step(V.tensor_scalar(lo_b[:, 1, :], local[0][:, :], -1.0, float(P), ALU.max, ALU.min))
            step(V.memset(pick[:, :, NB:PK], 1.0))
            dve.wait_ge(s_att, NB)
            rest = attn_rest[:, :, :, :]
            step(V.tensor_copy(rest, attn[:, :, :].rearrange("p n (s h) -> p s n h", s=2)))
            for c in range(3):
                step(V.tensor_copy(attn_part[:, :, c, :, :], rest))
                step(V.tensor_sub(rest, rest, attn_part[:, :, c, :, :]))
            V.memset(U, 0.0).then_inc(s_parts, 1)

            def destination_onehot(count, u):
                dve.wait_ge(s_bcast_dst, count + 1)
                dve.wait_ge(s_picked_mm, count + 1)
                V.tensor_scalar(onehotT_d[:, u, :], ps[:, 2:4, :].rearrange("p b c -> p (b c)")[:, 0:BLK * P],
                                part, None, ALU.is_equal).then_inc(s_onehot_dst, 1)

            def pick_logits(count, u):
                last = V.tensor_tensor(pick[:, :, 0:NB], iota[:, 0:NB].unsqueeze(1).to_broadcast([P, BLK, NB]),
                                       hi_f[:, 0, bass.ds(count * BLK, BLK)].unsqueeze(2).to_broadcast([P, BLK, NB]),
                                       ALU.is_equal)
                last.then_inc(s_pick, 1)
                dve.wait_ge(s_pick, count * 2 + 1)
                dve.wait_ge(s_picked_mm, count + 3)
                grid = ps[:, 4 + 2 * u:6 + 2 * u, :].rearrange("p b (j c) -> p (b j) c", c=P)[:, 0:BLK, 0:PK * H]
                V.tensor_tensor(picked.rearrange("p j (a h) -> p j a h", h=H), grid.rearrange("p j (a h) -> p j a h", h=H),
                                pick.unsqueeze(3).to_broadcast([P, BLK, PK, H]), ALU.mult).then_inc(s_pick, 1)
                hold(dve, s_pick, count * 2 + 2, s_tok_dve)
                V.reduce_sum(logit[:, bass.ds(count * BLK, BLK), :], picked.rearrange("p j (a h) -> p j h a", h=H),
                             axis=AX.X).then_inc(s_picked, 1)

            destination_onehot(0, 0)
            with dve.Fori(0, PAIRS) as i:
                for u in range(2):
                    destination_onehot(i * 2 + (u + 1), 1 - u)
                    pick_logits(i * 2 + u, u)
            pick_logits(2 * PAIRS, 0)
            dve.wait_ge(s_picked, NT // BLK + 2)
            step(V.scalar_tensor_tensor(out=logit, in0=logit, scalar=0.2, in1=logit, op0=ALU.mult, op1=ALU.max))
            step(V.tensor_tensor(logit, logit, slots[0][:, :, 3:4].to_broadcast([P, NT, H]), ALU.mult))
            step(V.tensor_scalar(off[:, :], local[0][:, :], 0.0, None, ALU.is_ge))
            step(V.scalar_tensor_tensor(out=off[:, :], in0=local[0][:, :], scalar=float(P), in1=off[:, :],
                                        op0=ALU.is_lt, op1=ALU.mult))
            step(V.tensor_scalar(off[:, :], off[:, :], FAR, -FAR, ALU.mult, ALU.add))
            step(V.tensor_tensor(logit, logit, off[:, :].unsqueeze(2).to_broadcast([P, NT, H]), ALU.add))
            V.reduce_max(mx[:, 0:1], logit.rearrange("p t h -> p (t h)"), axis=AX.X).then_inc(s_mx, 1)
            dve.wait_ge(s_mT, 1)
            step(V.reduce_max(mrow[0:1, 0:1], ps[0:1, 0, 0:P], axis=AX.X))
            V.tensor_scalar_mul(mrow[0:1, 1:2], mrow[0:1, 0:1], -1.0).then_inc(s_m1, 1)
            dve.wait_ge(s_mB, 1)
            V.tensor_copy(mx[:, 1:2], ps[:, 1, 0:1]).then_inc(s_negM, 1)
            dve.wait_ge(s_exp, 1)
            aggregate(1, 0)
            step(V.tensor_scalar_add(sc[:, :, :], U[:, :, F:F + H], 1e-10))
            step(V.reciprocal(sc[:, :, :], sc[:, :, :]))
            for h in range(H):
                cut = U[:, :, h * (F // H):(h + 1) * (F // H)]
                last = V.tensor_tensor(cut, cut, sc[:, :, h:h + 1].to_broadcast([P, NB, F // H]), ALU.mult)
            step(last)
            step(V.tensor_add(X[:, :, :], X[:, :, :], U[:, :, 0:F]))

            norm_stats(2)
            localise(1)
            take_rows(2)
            dve.wait_ge(s_h, 3 * NB)
            step(V.tensor_add(X[:, :, :], X[:, :, :], b2_b[:, :].unsqueeze(1).to_broadcast([P, NB, F])))
            aggregate(2, 1)

            norm_stats(3)
            take_rows(3)
            for g in range(PITERS):
                cut = slice(g * NG, (g + 1) * NG)
                s, e = sc[:, cut, :], sc2[:, cut, :]
                top, whole = sm[:, cut, 0], sm[:, cut, 1]
                dve.wait_ge(s_last[g], NG * 32)
                step(V.tensor_add(s, al[:, cut, :], final_rows[:, cut, F:F + H]))
                step(V.scalar_tensor_tensor(out=s, in0=s, scalar=0.01, in1=s, op0=ALU.mult, op1=ALU.max))
                step(V.reduce_max(top, s, axis=AX.X))
                V.tensor_tensor(s, s, sm[:, cut, 0:1].to_broadcast([P, NG, H]), ALU.subtract).then_inc(s_e3, 1)
                dve.wait_ge(s_e3x, g + 1)
                step(V.reduce_sum(whole, e, axis=AX.X))
                step(V.reciprocal(whole, whole))
                step(V.tensor_tensor(e, e, sm[:, cut, 1:2].to_broadcast([P, NG, H]), ALU.mult))
                for h in range(H):
                    r = final_rows[:, cut, h * (F // H):(h + 1) * (F // H)]
                    last = V.tensor_tensor(r, r, sc2[:, cut, h:h + 1].to_broadcast([P, NG, F // H]), ALU.mult)
                step(last)
                for h in range(1, H):
                    r = final_rows[:, cut, h * (F // H):(h + 1) * (F // H)]
                    step(V.tensor_add(final_rows[:, cut, 0:F // H], final_rows[:, cut, 0:F // H], r))
                for h in range(H):
                    xc = X[:, cut, h * (F // H):(h + 1) * (F // H)]
                    last = V.tensor_add(xc, xc, final_rows[:, cut, 0:F // H])
                last.then_inc(s_done, 1)

        @block.tensor
        def _(pe):
            mm = nc.tensor.matmul
            pe.sem_inc(s_tr, NG)
            pe.sem_inc(s_quarter, 4 * NG)
            pe.sem_inc(s_row, NG)
            pe.sem_inc(s_distance, 1)
            pe.sem_inc(s_onehot_dst, 1)
            pe.sem_inc(s_picked_mm, 2)

            def count_buckets(c):
                pe.wait_ge(s_member, c + 1)
                pe.wait_ge(s_offset, 1)
                if c:
                    pe.wait_ge(s_spread_out, 2)
                for b in range(NB):
                    if c or b:
                        pe.wait_ge(s_count_out, c * NB + b)
                    mm(ps[:, 0, 0:ET], ones_b[:, :], member[:, b, :], start=True, stop=True).then_inc(s_count, 1)
                    if c or b:
                        pe.wait_ge(s_before_out, c * NB + b)
                    mm(ps[:, 1, 0:ET], tri_b[:, :], member[:, b, :], start=True, stop=True).then_inc(s_before, 1)

            def spread_buckets(q):
                pe.wait_ge(s_sizes, q + 1)
                if q:
                    pe.wait_ge(s_before_out, NB)
                    pe.wait_ge(s_count_out, NB)
                for n, c in enumerate((3, 5)):
                    last = nc.tensor.transpose(ps[0:NB, 0, n * P:(n + 1) * P], total[:, q, c, :].unsqueeze(1).to_broadcast(
                        [P, 1, NB]).rearrange("p a b -> p (a b)"), ident)
                last.then_inc(s_spread, 1)
                pe.wait_ge(s_begun, q + 1)
                mm(ps[:, 0, 0:NT], ones_row[0:NB, 0:P], begun[:, :], start=True, stop=True)
                mm(ps[:, 1, 0:NT], spread[:, 1, :], begun[:, :], start=True, stop=True).then_inc(s_spread, 1)

            def project(l, start, end):
                c0 = l * NB
                W = (W0, W1, W2, W3)[l]
                wide = (2 * F, FW, F, FW)[l]

                def transpose(i, j):
                    pe.wait_ge(s_h, i * NG + (c0 + j + 1))
                    pe.wait_ge(s_hT, i * NG + (c0 + j + 1))
                    for k in range(KT):
                        last = nc.tensor.transpose(ps[:, 2 + j % 2, k * P:(k + 1) * P], h_ring[:, j, k * P:(k + 1) * P], ident)
                    last.then_inc(s_tr, 1)

                def products(i, j):
                    pe.wait_ge(s_hT, i * NG + (c0 + j + 2))
                    if l == 0:
                        for q in range(4):
                            pe.wait_ge(s_quarter_out, i * (4 * NG) + (4 * j + q + 1))
                            for k in range(KT):
                                last = mm(ps[:, 4 + q, :], hT_ring[:, j, k, :], W[:, k, q * wide:(q + 1) * wide],
                                          start=(k == 0), stop=(k == KT - 1))
                            last.then_inc(s_quarter, 1)
                    else:
                        bank = (4 + j) % 8
                        pe.wait_ge(s_row_out, i * NG + ((l - 1) * NB + j + 1))
                        for k in range(KT):
                            last = mm(ps[:, bank, 0:wide], hT_ring[:, j, k, :], W[:, k, :], start=(k == 0), stop=(k == KT - 1))
                        last.then_inc(s_row, 1)

                with pe.Fori(start, end) as i:
                    transpose(i, 0)
                    transpose(i, 1)
                    for j in range(NG):
                        products(i, j)
                        if j + 2 < NG:
                            transpose(i, j + 2)

            def aggregate(l):
                with pe.Fori(0, ITERS) as i:
                    for k in range(SETS):
                        blocks = i * SETS + (l * ITERS * SETS + k + 1)
                        tiles = i * RING + (l * NT + k * BLK)
                        pe.wait_ge(s_onehot, blocks)
                        if l == 0:
                            pe.wait_ge(s_rows[k], i * (BLK * 16) + BLK * 16)
                        else:
                            pe.wait_ge(s_scaled, i * SETS + ((l - 1) * ITERS * SETS + k + 1))
                        for j in range(BLK):
                            pe.wait_ge(s_added, tiles + (j + 1 - BLK + RING))
                            width = F + H if l == 1 else F
                            mm(ps[:, j, 0:width], onehot[:, k, j, :], rows[:, k * BLK + j, 0:width],
                               start=True, stop=True).then_inc(s_mm, 1)

            pe.wait_ge(s_constb, 3)
            pe.wait_ge(s_w, 128)
            project(0, 0, 1)
            pe.wait_ge(s_part, 1)
            mm(ps[:, 0, 0:NB], ones_row[:, 0:P], total[:, 0, 1, :], start=True, stop=True).then_inc(s_whole, 1)
            spread_buckets(0)
            count_buckets(0)
            project(0, 1, 2)
            spread_buckets(1)
            project(0, 2, 4)
            count_buckets(1)
            project(0, 4, PITERS)
            aggregate(0)
            project(1, 0, PITERS)
            pe.wait_ge(s_parts, 1)

            def broadcast_nodes(count, u):
                for s in range(2):
                    if s == 0:
                        pe.wait_ge(s_distance, count + 1)
                    else:
                        pe.wait_ge(s_onehot_dst, count + 1)
                    for j in range(BLK):
                        last = mm(ps[:, 2 * s + j // 4, (j % 4) * P:(j % 4 + 1) * P],
                                  lo_b[:, s, bass.ds(count * BLK + j, 1)].to_broadcast([P, P]), ident_b[:, :],
                                  start=True, stop=True)
                    last.then_inc(s_bcast_dst if s else s_bcast_src, 1)

            def look_up(count, u):
                _, buckets = nc.values_load_multi_w_load_instructions(
                    tile_bucket_i[0][0:1, bass.ds(count * BLK, BLK)], engines=[mybir.EngineType.PE],
                    min_val=0, max_val=NB - 1,
                    skip_runtime_bounds_check_because="a count of bucket starts less one, at most NB - 1")
                pe.wait_ge(s_onehot_src, count + 2)
                pe.wait_ge(s_onehot_dst, count + 2)
                pe.wait_ge(s_picked, count + 1)
                for j in range(BLK):
                    at = (j % 4) * P
                    for c in range(3):
                        mm(ps[:, 4 + 2 * u + j // 4, at:at + NB * H], onehotT_s[:, u, j * P:(j + 1) * P],
                           attn_part[:, 0, c, :, :].rearrange("p n h -> p (n h)"), start=(c == 0), stop=(c == 2))
                    for c in range(3):
                        last = mm(ps[:, 4 + 2 * u + j // 4, at + NB * H:at + PK * H], onehotT_d[:, u, j * P:(j + 1) * P],
                                  attn_part[:, 1, c, bass.ds(buckets[j], 1), :].rearrange("p n h -> p (n h)"),
                                  start=(c == 0), stop=(c == 2))
                last.then_inc(s_picked_mm, 1)

            broadcast_nodes(0, 0)
            with pe.Fori(0, PAIRS) as i:
                for u in range(2):
                    broadcast_nodes(i * 2 + (u + 1), 1 - u)
                    look_up(i * 2 + u, u)
            look_up(2 * PAIRS, 0)
            pe.wait_ge(s_mx, 1)
            nc.tensor.transpose(ps[0:1, 0, 0:P], mx[:, 0:1], ident).then_inc(s_mT, 1)
            pe.wait_ge(s_m1, 1)
            mm(ps[:, 1, 0:1], ones_row[0:1, 0:P], mrow[0:1, 1:2], start=True, stop=True).then_inc(s_mB, 1)
            aggregate(1)
            project(2, 0, PITERS)
            aggregate(2)
            project(3, 0, PITERS)


_OUT = ((P, NB, F), "float32")


def kernel(**inputs):
    import numpy as np
    import concourse.bacc as bacc
    from concourse.bass_utils import run_bass_kernel_spmd as run

    def nodes(a):
        a = np.pad(np.asarray(a), ((0, NB * P - N), (0, 0)))
        return a.reshape(NB, P, F).transpose(1, 0, 2)

    def edges(a, fill):
        a = np.pad(np.asarray(a), (0, ET * P - E), constant_values=fill)
        return a.reshape(ET, P).T

    def deep(a):
        return np.asarray(a).reshape(KT, P, -1).transpose(1, 0, 2)

    consts = np.zeros((P, CW), np.float32)
    consts[:, C_IOTA:C_IOTA + P] = np.arange(P)
    consts[:, C_ID:C_ID + P] = np.eye(P)
    consts[:, C_TRI:C_TRI + P] = -(np.arange(P)[:, None] >= np.arange(P)[None, :]).astype(np.float32)
    consts[:, C_SLOT:C_SLOT + NT] = np.arange(NT)
    consts[:, C_PART] = np.arange(P)
    consts[:, C_MINUS] = -np.arange(P)
    left = E - (ET - 1) * P
    consts[left:, C_PAD] = P * NT + np.arange(left, P)

    def edges_by_row(a, fill):
        return np.pad(np.asarray(a), (0, ET * P - E), constant_values=fill).reshape(P, ET)

    src, dst, kind = inputs["src"], inputs["dst"], inputs["edge_type_8"]
    arrays = {
        "x": nodes(inputs["x"]),
        "ecols": np.stack([edges(src, NB * P), edges(dst, NB * P), edges(kind, 0)], 1),
        "wcols": edges(inputs["edge_weight"], 0),
        "erows": np.stack([edges_by_row(src, 0), edges_by_row(dst, NB * P),
                           np.pad(np.asarray(dst)[1:], (0, ET * P - E + 1), constant_values=NB * P).reshape(P, ET),
                           edges_by_row(kind, 0)], 1),
        "wrows": edges_by_row(inputs["edge_weight"], 0),
        "consts": consts,
        "w0": deep(np.asarray(inputs["L0_gnn_weight"]).transpose(2, 0, 1).reshape(F, R * F)),
        "bias0": np.asarray(inputs["L0_gnn_bias"]).reshape(1, F),
        "w1": deep(np.asarray(inputs["L1_gnn_W"]).transpose(1, 0, 2).reshape(F, F)),
        "a1": np.stack([np.asarray(inputs["L1_gnn_a_src"]).reshape(F), np.asarray(inputs["L1_gnn_a_dst"]).reshape(F)]),
        "w2": deep(inputs["L2_gnn_W"]),
        "b2": np.asarray(inputs["L2_gnn_b"]).reshape(1, F),
        "w3": deep(inputs["L3_gnn_weight"]),
        "a3": np.stack([np.asarray(inputs["L3_gnn_attn_l"]).reshape(F), np.asarray(inputs["L3_gnn_attn_r"]).reshape(F)]),
    }
    nc = bacc.Bacc("TRN2", target_bir_lowering=False, num_devices=1)
    maps, args = {}, []
    for name, a in arrays.items():
        a = np.ascontiguousarray(a)
        maps[f"in_{name}"] = a
        args.append(nc.dram_tensor(f"in_{name}", a.shape, mybir.dt.from_np(a.dtype), kind="ExternalInput").ap())
    o = nc.dram_tensor("out_0", _OUT[0], F32, kind="ExternalOutput").ap()
    build(nc, *args, o)
    r = run(nc, [maps], core_ids=[0])
    got = r.results[0]["out_0"]
    return np.ascontiguousarray(got.transpose(1, 0, 2).reshape(NB * P, F)[:N])
```

```python
from contextlib import ExitStack

import concourse.bass as bass
from concourse import mybir

F32 = mybir.dt.float32
BF16 = mybir.dt.bfloat16
I32 = mybir.dt.int32
ALU = mybir.AluOpType
ACT = mybir.ActivationFunctionType
AX = mybir.AxisListType

P = 128
N, F, E, R, H = 3125, 256, 53125, 8, 4
NB = -(-N // P)
ET = -(-E // P)
NT = ET + NB
BLK = 7
SETS = 3
RING = BLK * SETS
ITERS = NT // RING
PARTS = [(k * BLK + a, k * BLK + b) for k in range(SETS) for a, b in ((0, 4), (4, BLK))]
NPART = len(PARTS)
assert NT == ITERS * RING
FW = F + 2 * H
RW = F + 8
CH = -(-ET // P)
CLAST = ET - (CH - 1) * P
TLAST = NT - NT // P * P
assert -(-NT // P) == CH
SH = 8
SITERS = ET // (2 * SH)
assert ET == SITERS * 2 * SH
NG = 5
PITERS = NB // NG
KT = F // P
EPS = 1e-5
FAR = 1e30

C_IOTA, C_ID, C_SLOT, C_PART, C_PAD = 0, P, 2 * P, 2 * P + NT, 2 * P + NT + 1
C_MINUS = C_PAD + 1
CW = C_MINUS + 1
FIRST_SCATTER = 11
LATE = 3
EARLY = 6
HALVES = ((0, EARLY * 2 * SH), (EARLY * 2 * SH, ET))

RUN = 32


def build(nc, x, ecols, wcols, erows, consts, w0, bias0, w1, a1, w2, b2, w3, a3, out):
    with ExitStack() as ctx:
        def sb(name, shape, dt=F32):
            return ctx.enter_context(nc.sbuf_tensor(name, shape, dt))

        def sem(name):
            return ctx.enter_context(nc.semaphore(name))

        def dram(name, shape, dt=F32):
            return nc.dram_tensor(name, shape, dt, kind="Internal").ap()

        table0_rows = dram("table0", [NB * P * R, F])
        table0 = table0_rows.rearrange("(n r) f -> n (r f)", r=R)
        tables = [None, dram("table1", [NB * P, F]), dram("table2", [NB * P, F]), dram("table3", [NB * P, FW])]
        last_rows = dram("last_rows", [NB * P], BF16)
        node_rows = dram("node_rows", [2, NT * P], BF16)
        slot_rows = [dram("slots_dst", [P * NT + P, 4]), dram("slots_src", [P * NT + P, 4])]

        X = sb("X", [P, NB, F])
        cst = sb("cst", [P, CW])
        iota, ident = cst[:, C_IOTA:C_IOTA + P], cst[:, C_ID:C_ID + P]
        minus_part = cst[:, C_MINUS:C_MINUS + 1]
        slot_no, part, pad_row = cst[:, C_SLOT:C_SLOT + NT], cst[:, C_PART:C_PART + 1], cst[:, C_PAD:C_PAD + 1]
        ident_b = sb("ident_b", [P, P], BF16)
        below_b = sb("below_b", [P, ET], BF16)
        ones_b = sb("ones_b", [P, P], BF16)
        ones_row = sb("ones_row", [P, ET])
        bias0_b = sb("bias0_b", [P, F])
        b2_b = sb("b2_b", [P, F])
        W1 = sb("W1", [P, KT, FW])
        W2 = sb("W2", [P, KT, F])
        W3 = sb("W3", [P, KT, FW])


        ecol = sb("ecol", [P, 3, ET], I32)
        wcol = sb("wcol", [P, ET])
        rec_d = sb("rec_d", [P, ET + RUN, 4])
        rec_s = sb("rec_s", [P, ET, 4])
        rank_f = sb("rank_f", [P, ET])
        run = sb("run", [P, ET])
        bucket_b = sb("bucket_b", [P, ET], BF16)
        count_b = sb("count_b", [P, CH, NB], BF16)
        tmp_i = sb("tmp_i", [P, NT], I32)
        tmp_j = sb("tmp_j", [P, ET], I32)
        place = [sb("place_dst", [P, ET], I32), sb("place_src", [P, ET], I32)]
        total = sb("total", [P, 2, 6, NB])
        total_i = sb("total_i", [P, NB], I32)
        tile_bucket = [sb("tile_bucket_d", [P, NT]), sb("tile_bucket_s", [P, NT])]
        tile_bucket_i = [sb("tile_bucket_di", [P, NT], I32), sb("tile_bucket_si", [P, NT], I32)]
        rec_ring = sb("rec_ring", [P, 2 * SH, 4])
        place_ring = sb("place_ring", [P, 2 * SH], I32)
        order_rec = sb("order_rec", [P, SH, 4])
        order_place = sb("order_place", [P, SH], I32)

        slots_wide = sb("slots_d", [P, NT + RUN, 4])
        slots = [slots_wide[:, 0:NT, :], rec_d[:, 0:NT, :]]
        local = [sb("local_d", [P, NT]), sb("local_s", [P, NT])]
        idx_ring = sb("idx_ring", [P, RING], I32)
        run_from = sb("run_from", [P, 2, NB], I32)
        spread = sb("spread", [NB, P])
        begun = sb("begun", [NB, NT])
        worst = sb("worst", [P, 4])
        unsorted_i = sb("unsorted_i", [P, 1], I32)

        sums_at = max(RING * RW, NT * (NB + 3) // 2 + 1)
        arena = sb("arena", [P, sums_at + NB * (F + H) + RING * P])
        member = arena[:, sums_at:sums_at + NB * ET // 2].bitcast(BF16).rearrange("p (b t) -> p b t", b=NB)
        assert NB * ET // 2 <= NB * (F + H)
        rows = arena[:, 0:RING * RW].rearrange("p (s f) -> p s f", s=RING)
        U = arena[:, sums_at:sums_at + NB * (F + H)].rearrange("p (n f) -> p n f", n=NB)
        final_rows = arena[:, 0:NB * FW].rearrange("p (n f) -> p n f", n=NB)
        oh_at = sums_at + NB * (F + H)
        onehot = arena[:, oh_at:oh_at + RING * P].rearrange("p (j c) -> p j c", j=RING)

        W0 = sb("W0", [P, KT, R * F])
        w0_flat = W0[:, :, :].rearrange("p k c -> p (k c)")
        logit = w0_flat[:, 0:NT * H].rearrange("p (t h) -> p t h", h=H)
        h_ring = sb("h_ring", [P, NG, F])
        hT_ring = sb("hT_ring", [P, NG, KT, P])
        out_ring = sb("out_ring", [P, 4, 2 * F])
        row_ring = arena[:, oh_at:oh_at + 2 * NG * FW].rearrange("p (j f) -> p j f", f=FW)
        assert 2 * NG * FW <= RING * P
        A1, A3, folded = row_ring[:, 1:3, 0:F], row_ring[:, 3:5, 0:F], row_ring[:, 0, 0:F]
        stats = sb("stats", [P, NB, 6])
        mean_var = sb("mean_var", [P, NB, 2])
        rstd = sb("rstd", [P, NB])
        shift = sb("shift", [P, NB])

        attn = sb("attn", [P, NB, 2 * H])
        attn_rest = sb("attn_rest", [P, 2, NB, H])
        attn_part = sb("attn_part", [P, 3, NB, H], BF16)
        attn_part_d = sb("attn_part_d", [P, NB, 3, H], BF16)
        lo_b = sb("lo_b", [P, 2, NT], BF16)
        hi_b = sb("hi_b", [P, NT], BF16)
        hi_f = sb("hi_f", [P, 1, NT])
        out_flat = out_ring[:, :, :].rearrange("p q c -> p (q c)")
        PK = NB + 3
        picked = [room[:, at:at + BLK * PK * H].rearrange("p (j c) -> p j c", j=BLK)
                  for room, at in ((out_flat, 0), (out_flat, BLK * PK * H), (h_ring[:, :, :].rearrange("p j c -> p (j c)"), 0))]
        pick = arena[:, 0:NT * PK // 2 + 1].bitcast(BF16)[:, 0:NT * PK].rearrange("p (b t) -> p b t", b=PK)
        wide_T = BLK * P
        onehotT = [w0_flat[:, NT * H + u * wide_T:NT * H + (u + 1) * wide_T].bitcast(BF16) for u in range(2)]
        onehotT.append(hT_ring[:, :, :, :].rearrange("p j k c -> p (j k c)")[:, 0:wide_T].bitcast(BF16))
        distance = [room[:, at:at + wide_T // 2].bitcast(BF16) for room, at in (
            (w0_flat, NT * H + 2 * wide_T), (out_flat, 2 * BLK * PK * H),
            (h_ring[:, :, :].rearrange("p j c -> p (j c)"), BLK * PK * H))]
        numbers = arena[:, oh_at:oh_at + RING * P].bitcast(BF16).rearrange("p (k s c) -> p k s c", k=SETS, s=2)
        last_at = NB * FW
        last_numbers, last_onehots = (arena[:, last_at + n * NB * P // 2:last_at + (n + 1) * NB * P // 2].bitcast(BF16)
                                      for n in range(2))
        last_chosen = arena[:, last_at + NB * P:last_at + NB * P + NB * NB * H].rearrange("p (j c) -> p j c", j=NB)
        assert sums_at <= last_at and last_at + NB * P + NB * NB * H <= oh_at
        last_lo = sb("last_lo", [P, NB], BF16)
        last_T = sb("last_T", [NB, P], BF16)
        last_pick = sb("last_pick", [P, NB, NB], BF16)
        last_hi = sb("last_hi", [P, 1, NB])
        lo_T = sb("lo_T", [P, 2, CH, P], BF16)
        off = sb("off", [P, NT])
        row_dst, row_next = local[0][:, 0:ET].bitcast(I32), local[1][:, 0:ET].bitcast(I32)
        mx = sb("mx", [P, 4])
        zero = sb("zero", [P, 1])
        mrow = sb("mrow", [1, 4])
        al = sb("al", [P, NB, H])
        sc = sb("sc", [P, NB, H])
        sc2 = sb("sc2", [P, NB, H])
        sm = sb("sm", [P, NB, 2])

        ps = ctx.enter_context(nc.psum_tensor("ps", [P, 8, 512], F32))

        s_cst = sem("s_cst")
        s_in = sem("s_in")
        s_src = sem("s_src")
        s_x = sem("s_x")
        s_w0, s_w = sem("s_w0"), sem("s_w")
        s_prep = sem("s_prep")
        s_prep_order = sem("s_prep_order")
        s_constb = sem("s_constb")
        s_member = sem("s_member")
        s_count = sem("s_count")
        s_count_out = sem("s_count_out")
        s_size = sem("s_size")
        s_rank = sem("s_rank")
        s_ranked = sem("s_ranked")
        s_rec_s = sem("s_rec_s")
        s_blank = sem("s_blank")
        s_blanked = sem("s_blanked")
        s_place = sem("s_place")
        s_recs = sem("s_recs")
        s_scat = [sem(f"s_scat{h}") for h in range(2)]
        s_slots = sem("s_slots")
        s_var = sem("s_var")
        s_sd = sem("s_sd")
        s_norm = sem("s_norm")
        s_h = sem("s_h")
        s_tr = sem("s_tr")
        s_hT = sem("s_hT")
        s_quarter = sem("s_quarter")
        s_quarter_out = sem("s_quarter_out")
        s_quarter_free = sem("s_quarter_free")
        s_store0 = [sem(f"s_store0_{q}") for q in range(4)]
        s_row = sem("s_row")
        s_row_out = sem("s_row_out")
        s_store = [sem(f"s_store{u}") for u in range(2)]
        s_last_lo, s_last_store = sem("s_last_lo"), sem("s_last_store")
        s_last_numbers = sem("s_last_numbers")
        s_last_onehots = sem("s_last_onehots")
        s_last_parts = sem("s_last_parts")
        s_last_picked = sem("s_last_picked")
        s_idx = sem("s_idx")
        s_rows = [sem(f"s_rows{g}") for g in range(NPART)]
        s_onehot = sem("s_onehot")
        s_scaled = sem("s_scaled")
        s_mm = sem("s_mm")
        s_added = sem("s_added")
        s_att = sem("s_att")
        s_zero = sem("s_zero")
        s_parts = sem("s_parts")
        s_lo, s_lo_mm, s_lo_out = sem("s_lo"), sem("s_lo_mm"), sem("s_lo_out")
        s_lo_store = sem("s_lo_store")
        s_numbers = [sem(f"s_numbers{k}") for k in range(SETS)]
        s_distance = sem("s_distance")
        s_onehots_src = sem("s_onehots_src")
        s_onehots_dst = sem("s_onehots_dst")
        s_picked_mm = sem("s_picked_mm")
        s_pick = sem("s_pick")
        s_picked = sem("s_picked")
        s_rec_d = sem("s_rec_d")
        s_run = sem("s_run")
        s_worst = sem("s_worst")
        s_sorted = sem("s_sorted")
        s_order = sem("s_order")
        s_ordered = sem("s_ordered")
        s_dst_slots = sem("s_dst_slots")
        s_sizes = sem("s_sizes")
        s_spread = sem("s_spread")
        s_begun = sem("s_begun")
        s_spread_out = sem("s_spread_out")
        s_mx = sem("s_mx")
        s_mT = sem("s_mT")
        s_m1 = sem("s_m1")
        s_mB = sem("s_mB")
        s_negM = sem("s_negM")
        s_exp = sem("s_exp")
        s_last = [sem(f"s_last{g}") for g in range(PITERS)]
        s_e3 = sem("s_e3")
        s_e3x = sem("s_e3x")
        s_done = sem("s_done")
        s_out = sem("s_out")
        s_tok_act = sem("s_tok_act")
        s_tok_sp = sem("s_tok_sp")
        s_tok_pool = sem("s_tok_pool")
        s_tok_dve = sem("s_tok_dve")
        s_tok_pe = sem("s_tok_pe")

        def stored(groups, u):
            return (groups + 1 - u) // 2

        def hold(eng, s, value, token):
            eng.wait_ge(s, value)
            eng.sem_inc(token, 1)

        block = ctx.enter_context(nc.Block())

        @block.sync
        def _(sp):
            sp.dma_start(ecol[:, 0, :], ecols[:, 0, :]).then_inc(s_src, 16)
            sp.dma_start(cst[:, :], consts).then_inc(s_cst, 16)
            sp.dma_start(ecol[:, 1:3, :], ecols[:, 1:3, :]).then_inc(s_in, 16)
            sp.dma_start(wcol[:, :], wcols).then_inc(s_in, 16)
            for n, dst in enumerate((row_dst, row_next)):
                sp.dma_start(dst, erows[:, n, :]).then_inc(s_in, 16)
            sp.dma_start(X[:, :, :], x).then_inc(s_x, 16)
            sp.dma_start(W0[:, :, :], w0).then_inc(s_w0, 16)
            for dst, src in ((W1[:, :, 0:F], w1), (W2[:, :, :], w2), (W3[:, :, 0:F], w3)):
                sp.dma_start(dst, src).then_inc(s_w, 16)
            for dst, src in ((A1, a1), (A3, a3)):
                sp.dma_start(dst, src.unsqueeze(0).to_broadcast([P, 2, F])).then_inc(s_w, 16)
            for dst, src in ((bias0_b, bias0), (b2_b, b2)):
                sp.dma_start(dst[:, :], src.to_broadcast([P, F])).then_inc(s_w, 16)
            sp.wait_ge(s_blank, 1)
            for q in range(2):
                sp.dma_start(slot_rows[q][0:P * NT, :].rearrange("(p t) c -> p (t c)", p=P),
                             slots[0].rearrange("p t c -> p (t c)")).then_inc(s_blanked, 16)
            def load_src_slots():
                for h in range(2):
                    sp.wait_ge(s_scat[h], SITERS * SH * 16)
                sp.dma_start(slots[1].rearrange("p t c -> p (t c)"),
                             slot_rows[1][0:P * NT, :].rearrange("(p t) c -> p (t c)", p=P)).then_inc(s_slots, 16)

            for q in range(4):
                sp.wait_ge(s_quarter_out, 4 + q + 1)
                sp.dma_start(table0[0:P, q * 2 * F:(q + 1) * 2 * F], out_ring[:, q, :]).then_inc(s_store0[q], 16)
            with sp.Fori(1, NB) as n:
                for q in range(4):
                    sp.wait_ge(s_store0[q], n * 16)
                    sp.sem_inc(s_quarter_free, 1)
                    hold(sp, s_quarter_out, n * 4 + (4 + q + 1), s_tok_sp)
                    sp.dma_start(table0[bass.ds(n * P, P), q * 2 * F:(q + 1) * 2 * F],
                                 out_ring[:, q, :]).then_inc(s_store0[q], 16)

            def store_rows(l):
                wide = FW if l == 3 else F
                for g in range(PITERS):
                    group = (l - 1) * PITERS + g
                    u = group % 2
                    sp.wait_ge(s_row_out, (group + 1) * NG + NG)
                    at = slice(g * NG * P, (g + 1) * NG * P)
                    sp.dma_start(tables[l][at, :].rearrange("(j p) f -> p j f", p=P),
                                 row_ring[:, u * NG:(u + 1) * NG, 0:wide]).then_inc(s_store[u], 16)

            sp.wait_ge(s_lo_out, 5)
            sp.dma_start(last_rows.rearrange("(t p) -> t p", p=P), last_T[:, :]).then_inc(s_last_store, 16)
            for s in range(2):
                sp.dma_start(node_rows[s, 0:(CH - 1) * P * P].rearrange("(c t p) -> t c p", c=CH - 1, p=P),
                             lo_T[:, s, 0:CH - 1, :]).then_inc(s_lo_store, 16)
                sp.dma_start(node_rows[s, (CH - 1) * P * P:NT * P].rearrange("(t p) -> t p", p=P),
                             lo_T[0:TLAST, s, CH - 1, :]).then_inc(s_lo_store, 16)
            store_rows(1)
            sp.wait_ge(s_lo_store, 4 * 16)
            for u in range(2):
                sp.wait_ge(s_store[u], stored(PITERS, u) * 16)
            with sp.Fori(0, ITERS) as i:
                for k in range(SETS):
                    hold(sp, s_distance, i * SETS + (k + 1), s_tok_sp)
                    hold(sp, s_onehots_dst, i * SETS + (k + 1), s_tok_sp)
                    sp.dma_start(numbers[:, k, :, :],
                                 node_rows[:, bass.ds(i * (RING * P) + k * (BLK * P), BLK * P)].unsqueeze(0).to_broadcast(
                                     [P, 2, BLK * P])).then_inc(s_numbers[k], 16)
            store_rows(2)
            load_src_slots()
            sp.wait_ge(s_last_store, 16)
            sp.wait_ge(s_norm, 2 + 2 * PITERS)
            sp.dma_start(last_numbers, last_rows.unsqueeze(0).to_broadcast([P, NB * P])).then_inc(s_last_numbers, 16)
            store_rows(3)
            for g in range(PITERS):
                sp.wait_ge(s_done, g + 1)
                sp.dma_start(out[:, g * NG:(g + 1) * NG, :], X[:, g * NG:(g + 1) * NG, :]).then_inc(s_out, 16)
            sp.wait_ge(s_out, PITERS * 16)

        @block.gpsimd
        def _(pool):
            def scatter_half(i, h):
                cut = bass.ds(i * (2 * SH) + h * SH, SH)
                nc.gpsimd.tensor_copy(rec_ring[:, h * SH:(h + 1) * SH, :], rec_s[:, cut, :]).then_inc(s_recs, 1)
                nc.gpsimd.tensor_copy(place_ring[:, h * SH:(h + 1) * SH], place[1][:, cut]).then_inc(s_recs, 1)
                hold(pool, s_recs, i * 4 + (2 * h + 2), s_tok_pool)
                for j in range(h * SH, (h + 1) * SH):
                    nc.gpsimd.indirect_dma_start(
                        out=slot_rows[1], out_offset=bass.IndirectOffsetOnAxis(ap=place_ring[:, j:j + 1], axis=0),
                        in_=rec_ring[:, j, :], in_offset=None).then_inc(s_scat[h], 16)

            def scatter(start, end):
                with pool.Fori(start, end) as i:
                    for h in range(2):
                        hold(pool, s_scat[h], i * (SH * 16), s_tok_pool)
                        scatter_half(i, h)

            def order_dst():
                pool.wait_ge(s_place, 4)
                pool.sem_inc(s_tok_pool, 1)
                with pool.Fori(0, ET // SH) as i:
                    nc.gpsimd.tensor_copy(order_rec[:, :, :], rec_d[:, bass.ds(i * SH, SH), :]).then_inc(s_order, 1)
                    nc.gpsimd.tensor_copy(order_place[:, :], place[0][:, bass.ds(i * SH, SH)]).then_inc(s_order, 1)
                    hold(pool, s_order, i * 2 + 2, s_tok_pool)
                    for j in range(SH):
                        nc.gpsimd.indirect_dma_start(
                            out=slot_rows[0], out_offset=bass.IndirectOffsetOnAxis(ap=order_place[:, j:j + 1], axis=0),
                            in_=order_rec[:, j, :], in_offset=None).then_inc(s_ordered, 16)
                    hold(pool, s_ordered, i * (SH * 16) + SH * 16, s_tok_pool)
                pool.dma_start(slots[0].rearrange("p t c -> p (t c)"),
                               slot_rows[0][0:P * NT, :].rearrange("(p t) c -> p (t c)", p=P)).then_inc(s_ordered, 16)
                pool.wait_ge(s_ordered, (ET + 1) * 16)

            def gather(l, table):
                with pool.Fori(0, ITERS) as i:
                    for k in range(SETS):
                        hold(pool, s_idx, i * SETS + (l * ITERS * SETS + k + 1), s_tok_pool)
                        for g in (2 * k, 2 * k + 1):
                            for j in range(*PARTS[g]):
                                nc.gpsimd.indirect_dma_start(
                                    out=rows[:, j, 0:F], out_offset=None, in_=table,
                                    in_offset=bass.IndirectOffsetOnAxis(ap=idx_ring[:, j:j + 1], axis=0)).then_inc(s_rows[g], 16)

            pool.wait_ge(s_worst, 1)
            nc.gpsimd.partition_all_reduce(worst[:, 1:2], worst[:, 0:1], P, bass.bass_isa.ReduceOp.max).then_inc(s_sorted, 1)
            pool.wait_ge(s_sorted, 1)
            pool.wait_ge(s_place, 1)
            pool.wait_ge(s_rec_s, 4)
            pool.wait_ge(s_blanked, 32)
            pool.sem_inc(s_tok_pool, 1)
            scatter_half(0, 0)
            scatter_half(0, 1)
            scatter(1, EARLY)
            pool.wait_ge(s_place, 2)
            pool.sem_inc(s_tok_pool, 1)
            scatter(EARLY, FIRST_SCATTER)
            pool.wait_ge(s_sizes, 2)
            pool.wait_ge(s_rec_d, 2)
            pool.wait_ge(s_blanked, 32)
            pool.sem_inc(s_tok_pool, 1)
            is_unsorted = pool.value_load(unsorted_i[0:1, 0:1], min_val=0, max_val=1)
            for b0 in range(0, NB, NG):
                _, edge_tiles = nc.values_load_multi_w_load_instructions(
                    run_from[0:1, 0, b0:b0 + NG], engines=[mybir.EngineType.Pool], min_val=0, max_val=ET,
                    skip_runtime_bounds_check_because="a count of edges in tiles, at most ET")
                _, slot_tiles = nc.values_load_multi_w_load_instructions(
                    run_from[0:1, 1, b0:b0 + NG], engines=[mybir.EngineType.Pool], min_val=0, max_val=NT,
                    skip_runtime_bounds_check_because="a count of slot tiles, at most NT")
                for n in range(NG):
                    nc.gpsimd.tensor_copy(slots_wide[:, bass.ds(slot_tiles[n], RUN), :],
                                          rec_d[:, bass.ds(edge_tiles[n], RUN), :]).then_inc(s_run, 1)
                    pool.wait_ge(s_run, b0 + n + 1)
            with pool.If(is_unsorted):
                order_dst()
            pool.sem_inc(s_dst_slots, 1)
            for q in range(4):
                pool.wait_ge(s_store0[q], NB * 16)
            pool.sem_inc(s_tok_pool, 1)
            gather(0, table0_rows)
            scatter(FIRST_SCATTER, SITERS - LATE)
            for l in (1, 2):
                for u in range(2):
                    pool.wait_ge(s_store[u], stored(l * PITERS, u) * 16)
                gather(l, tables[l])
                if l == 1:
                    scatter(SITERS - LATE, SITERS)
            for u in range(2):
                pool.wait_ge(s_store[u], stored(3 * PITERS, u) * 16)
            for n in range(NB):
                g = n // NG
                nc.gpsimd.indirect_dma_start(
                    out=final_rows[:, n, :], out_offset=None, in_=tables[3],
                    in_offset=bass.IndirectOffsetOnAxis(ap=ecol[:, 1, n:n + 1], axis=0)).then_inc(s_last[g], 16)

        @block.scalar
        def _(act):
            act.sem_inc(s_hT, 1)
            act.sem_inc(s_quarter_out, 4)
            act.sem_inc(s_quarter_free, 4)
            act.sem_inc(s_distance, SETS)
            act.sem_inc(s_onehots_src, SETS)
            act.wait_ge(s_cst, 16)
            nc.scalar.copy(ident_b[:, :], ident).then_inc(s_constb, 1)

            def project(l):
                c0 = l * NB

                def root(i):
                    hold(act, s_var, i + ((l - 1) * PITERS + 3), s_tok_act)
                    nc.scalar.activation(rstd[:, bass.ds(i * NG, NG)], mean_var[:, bass.ds(i * NG, NG), 1],
                                         ACT.Sqrt).then_inc(s_sd, 1)

                def normalise(i, j):
                    hold(act, s_tr, i * NG + (c0 + j + 1), s_tok_act)
                    n = i * NG + j
                    nc.scalar.activation(h_ring[:, j, :].unsqueeze(1), X[:, bass.ds(n, 1), :], ACT.Relu,
                                         bias=shift[:, bass.ds(n, 1)], scale=rstd[:, bass.ds(n, 1)]).then_inc(s_h, 1)

                def take_transposed(i, j):
                    act.wait_ge(s_tr, i * NG + (c0 + j + 1 + NG))
                    if l == 0:
                        hold(act, s_quarter, i * (4 * NG) + (4 * j + 4), s_tok_act)
                    else:
                        hold(act, s_row, i * NG + (c0 - NB + j + 1), s_tok_act)
                    nc.scalar.copy(hT_ring[:, j, :, :].rearrange("p k n -> p (k n)"),
                                   ps[:, 2 + j % 2, 0:F]).then_inc(s_hT, 1)

                def take_quarters(i, j):
                    for q in range(4):
                        act.wait_ge(s_quarter, i * (4 * NG) + (4 * j + q + 1 + 4 * NG))
                        hold(act, s_quarter_free, i * (4 * NG) + (4 * j + q + 1), s_tok_act)
                        nc.scalar.copy(out_ring[:, q, :], ps[:, 4 + q, :]).then_inc(s_quarter_out, 1)

                def turn(i, more):
                    if l:
                        hold(act, s_norm, i + ((l - 1) * PITERS + 3), s_tok_act)
                    normalise(i, 0)
                    normalise(i, 1)
                    take_transposed(i, 0)
                    for j in range(NG):
                        if j + 2 < NG:
                            normalise(i, j + 2)
                        if j + 1 < NG:
                            take_transposed(i, j + 1)
                        if j == 1 and more:
                            root(i + 1)
                        if l == 0:
                            take_quarters(i, j)

                if l == 0:
                    act.wait_ge(s_var, 1)
                    nc.scalar.activation(rstd[:, 0:NG], mean_var[:, 0:NG, 1], ACT.Sqrt).then_inc(s_sd, 1)
                    act.wait_ge(s_norm, 1)
                    turn(0, False)
                    act.wait_ge(s_var, 2)
                    nc.scalar.activation(rstd[:, NG:NB], mean_var[:, NG:NB, 1], ACT.Sqrt).then_inc(s_sd, 1)
                    act.wait_ge(s_norm, 2)
                    with act.Fori(1, PITERS) as i:
                        turn(i, False)
                else:
                    root(0)
                    with act.Fori(0, PITERS - 1) as i:
                        turn(i, True)
                    turn(PITERS - 1, False)

            def copy_indices(l, q):
                if q == 0:
                    act.wait_ge(s_dst_slots, 1)
                else:
                    act.wait_ge(s_slots, 16)
                with act.Fori(0, ITERS) as i:
                    for k in range(SETS):
                        hold(act, s_added, i * RING + (l * NT + (k + 1) * BLK), s_tok_act)
                        nc.scalar.copy(idx_ring[:, k * BLK:(k + 1) * BLK],
                                       slots[q][:, bass.ds(i * RING + k * BLK, BLK), 1 if l == 1 else 0]).then_inc(s_idx, 1)

            act.wait_ge(s_src, 16)
            act.wait_ge(s_in, 4 * 16)
            nc.scalar.copy(rec_s[:, :, 0], ecol[:, 1, :]).then_inc(s_rec_s, 1)
            nc.scalar.copy(rec_s[:, :, 2], ecol[:, 0, :]).then_inc(s_rec_s, 1)
            nc.scalar.copy(rec_s[:, :, 3], wcol[:, :]).then_inc(s_rec_s, 1)
            nc.scalar.copy(rec_d[:, 0:ET, 2], ecol[:, 1, :])
            nc.scalar.copy(rec_d[:, 0:ET, 3], wcol[:, :])
            act.wait_ge(s_blank, 1)
            nc.scalar.copy(rec_d[:, ET:ET + RUN, :], slots_wide[:, 0:RUN, :]).then_inc(s_rec_d, 1)
            project(0)
            copy_indices(0, 0)
            project(1)
            act.wait_ge(s_lo, 1)
            nc.scalar.copy(U.rearrange("p n f -> p (n f)"), zero[:, :].to_broadcast([P, NB * (F + H)])).then_inc(s_zero, 1)

            def source_distance(i, k):
                act.wait_ge(s_numbers[k], i * 16 + 16)
                hold(act, s_onehots_src, i * SETS + (k + 1), s_tok_act)
                nc.scalar.activation(distance[k], numbers[:, k, 0, :], ACT.Abs,
                                     bias=minus_part).then_inc(s_distance, 1)

            def source_onehots(i, k):
                act.wait_ge(s_distance, i * SETS + (k + 1 + SETS))
                hold(act, s_picked_mm, i * SETS + (k + 1), s_tok_act)
                nc.scalar.activation(onehotT[k][:, 0:wide_T], distance[k], ACT.Relu, bias=1.0,
                                     scale=-1.0).then_inc(s_onehots_src, 1)

            source_distance(0, 0)
            with act.Fori(0, ITERS - 1) as i:
                for k in range(SETS):
                    source_distance(i + (k + 1) // SETS, (k + 1) % SETS)
                    source_onehots(i, k)
            for k in range(SETS):
                if k + 1 < SETS:
                    source_distance(ITERS - 1, k + 1)
                source_onehots(ITERS - 1, k)
            act.wait_ge(s_negM, 1)
            nc.scalar.activation(logit, logit, ACT.Exp, bias=mx[:, 1:2]).then_inc(s_exp, 1)
            copy_indices(1, 0)
            project(2)
            copy_indices(2, 1)
            project(3)
            for g in range(PITERS):
                act.wait_ge(s_e3, g + 1)
                cut = slice(g * NG, (g + 1) * NG)
                nc.scalar.activation(sc2[:, cut, :], sc[:, cut, :], ACT.Exp).then_inc(s_e3x, 1)

        @block.vector
        def _(dve):
            done, done_order = [0], [0]

            def step(ins):
                done[0] += 1
                ins.then_inc(s_prep, 1)
                dve.wait_ge(s_prep, done[0])

            def step_order(ins):
                done_order[0] += 1
                ins.then_inc(s_prep_order, 1)
                dve.wait_ge(s_prep_order, done_order[0])

            V = nc.vector
            dve.sem_inc(s_added, RING)
            dve.sem_inc(s_row_out, NG)
            dve.sem_inc(s_picked, SETS)
            dve.sem_inc(s_onehots_dst, SETS)
            V.memset(ones_b[:, :], 1.0).then_inc(s_constb, 1)
            step(V.memset(ones_row[:, :], 1.0))
            step(V.memset(zero[:, :], 0.0))
            step(V.memset(slots_wide[:, :, :], 0.0))
            V.memset(slots_wide[:, :, 2:3], -1.0).then_inc(s_blank, 1)

            def norm_stats(l, g0, g1):
                group = slice(g0 * NG, g1 * NG)
                for n in range(g0 * NG, g1 * NG):
                    last = V.bn_stats(stats[:, n, :], X[:, n, :])
                step(last)
                for n in range(g0 * NG, g1 * NG):
                    last = V.bn_aggr(mean_var[:, n, :], stats[:, n, :])
                step(last)
                V.tensor_scalar_add(mean_var[:, group, 1], mean_var[:, group, 1], EPS).then_inc(s_var, 1)
                dve.wait_ge(s_sd, 2 + (l - 1) * PITERS + g1 if l else 1 + (g0 > 0))
                step(V.reciprocal(rstd[:, group], rstd[:, group]))
                V.scalar_tensor_tensor(out=shift[:, group], in0=mean_var[:, group, 0], scalar=-1.0, in1=rstd[:, group],
                                       op0=ALU.mult, op1=ALU.mult).then_inc(s_norm, 1)

            def mark_members(q):
                step(V.tensor_scalar(tmp_j[:, :], ecol[:, 1 - q, :], 7, None, ALU.arith_shift_right))
                step(V.tensor_copy(bucket_b[:, :], tmp_j[:, :]))
                for b in range(NB):
                    last = V.tensor_scalar(member[:, b, :], bucket_b[:, :], float(b), None, ALU.is_equal)
                return last

            def take_counts(q):
                c = 1 - q
                dve.wait_ge(s_count, c + 1)
                V.tensor_copy(count_b[:, 0:CH - 1, :].rearrange("p c b -> p (c b)"),
                              ps[:, 0, 0:(CH - 1) * NB]).then_inc(s_count_out, 1)
                V.tensor_copy(count_b[0:CLAST, CH - 1, :], ps[0:CLAST, 0, (CH - 1) * NB:CH * NB]).then_inc(s_count_out, 1)
                dve.wait_ge(s_size, c + 1)
                step(V.tensor_copy(total[:, q, 0, :], ps[:, 1, 0:NB]))

            def place_buckets(q):
                size, tiles, upto, first, start, edge_tile = (total[:, q, c, :] for c in range(6))
                step(V.tensor_scalar_add(start, size, float(P - 1)))
                step(V.tensor_copy(total_i[:, :], start))
                step(V.tensor_scalar(total_i[:, :], total_i[:, :], 7, None, ALU.arith_shift_right))
                step(V.tensor_copy(tiles, total_i[:, :]))
                if q == 0:
                    touched, less = worst[:, 2:3], worst[:, 1:2]
                    step(V.tensor_tensor_scan(upto, ones_row[:, 0:NB], size, 0.0, ALU.mult, ALU.add))
                    step(V.tensor_sub(first, upto, size))
                    step(V.tensor_copy(total_i[:, :], first))
                    step(V.tensor_scalar(total_i[:, :], total_i[:, :], 7, None, ALU.arith_shift_right))
                    step(V.tensor_copy(edge_tile, total_i[:, :]))
                    step(V.tensor_copy(run_from[:, 0, :], edge_tile))
                    step(V.tensor_scalar_add(upto, upto, float(P - 1)))
                    step(V.tensor_copy(total_i[:, :], upto))
                    step(V.tensor_scalar(total_i[:, :], total_i[:, :], 7, None, ALU.arith_shift_right))
                    step(V.tensor_copy(upto, total_i[:, :]))
                    step(V.tensor_sub(upto, upto, edge_tile))
                    dve.wait_ge(s_sorted, 1)
                    step(V.reduce_max(touched, upto, axis=AX.X))
                    step(V.tensor_scalar(touched, touched, float(RUN), None, ALU.is_gt))
                    step(V.tensor_scalar(less, less, 0.0, None, ALU.is_gt))
                    step(V.tensor_max(less, less, touched))
                    step(V.tensor_copy(unsorted_i[:, :], less))
                    step(V.tensor_sub(tiles, tiles, upto))
                    step(V.tensor_scalar(tiles, tiles, less, None, ALU.mult))
                    step(V.tensor_add(tiles, tiles, upto))
                step(V.tensor_tensor_scan(upto, ones_row[:, 0:NB], tiles, 0.0, ALU.mult, ALU.add))
                step(V.tensor_sub(first, upto, tiles))
                if q == 0:
                    step(V.tensor_copy(run_from[:, 1, :], first))
                V.tensor_scalar_mul(start, first, float(P)).then_inc(s_sizes, 1)
                dve.wait_ge(s_sizes, 2 - q)

            def spread_buckets(q):
                c = 1 - q
                dve.wait_ge(s_spread, 2 * c + 1)
                step(V.tensor_copy(spread[:, :], ps[0:NB, 0, 0:P]))
                V.tensor_scalar(begun[:, :], slot_no[0:NB, :], spread[:, 0:1], None, ALU.is_ge).then_inc(s_begun, 1)
                dve.wait_ge(s_spread, 2 * c + 2)
                step(V.tensor_scalar_add(tile_bucket[q][:, :], ps[:, 0, 0:NT], -1.0))
                V.tensor_copy(tile_bucket_i[q][:, :], tile_bucket[q][:, :]).then_inc(s_spread_out, 1)

            def rank_edges(q, half):
                one = step if q else step_order
                start = total[:, q, 4, :]
                t0, t1 = HALVES[half]
                edges = slice(t0, t1)
                one(V.memset(rank_f[:, edges], 0.0))
                for b in range(NB):
                    m = half * NB + b
                    dve.wait_ge(s_rank, (1 - q) * 2 * NB + m + 1)
                    V.scalar_tensor_tensor(out=run[:, edges], in0=ps[:, m % 2, edges], scalar=start[:, b:b + 1],
                                           in1=member[:, b, edges], op0=ALU.add, op1=ALU.mult).then_inc(s_ranked, 1)
                    dve.wait_ge(s_ranked, (1 - q) * 2 * NB + m + 1)
                    one(V.tensor_add(rank_f[:, edges], rank_f[:, edges], run[:, edges]))
                one(V.tensor_copy(place[q][:, edges], rank_f[:, edges]))
                one(V.tensor_scalar(tmp_j[:, edges], place[q][:, edges], P - 1, None, ALU.bitwise_and))
                one(V.tensor_copy(run[:, edges], tmp_j[:, edges]))
                one(V.tensor_scalar(tmp_j[:, edges], place[q][:, edges], 7, None, ALU.arith_shift_right))
                one(V.scalar_tensor_tensor(out=rank_f[:, edges], in0=run[:, edges], scalar=float(NT),
                                            in1=tmp_j[:, edges], op0=ALU.mult, op1=ALU.add))
                if t1 == ET:
                    one(V.tensor_add(rank_f[:, ET - 1:ET], rank_f[:, ET - 1:ET], pad_row))
                V.tensor_copy(place[q][:, edges], rank_f[:, edges]).then_inc(s_place, 1)

            def localise(q):
                dve.wait_ge(s_slots if q else s_dst_slots, 16 if q else 1)
                step(V.scalar_tensor_tensor(out=local[q][:, :], in0=tile_bucket[q][:, :], scalar=-float(P),
                                            in1=slots[q][:, :, 2], op0=ALU.mult, op1=ALU.add))

            def aggregate(l, q):
                width = F + H if l == 1 else F
                into = U if l == 1 else X

                def one_onehot(i, g, j):
                    made = V.tensor_tensor(onehot[:, j, :], iota,
                                           local[q][:, bass.ds(i * RING + j, 1)].to_broadcast([P, P]), ALU.is_equal)
                    if j == PARTS[g][1] - 1:
                        made.then_inc(s_onehot, 1)

                def weigh(i, g):
                    if l == 0:
                        return
                    j0, j1 = PARTS[g]
                    n = j1 - j0
                    dve.wait_ge(s_rows[g], i * (n * 16) + (l * ITERS + 1) * n * 16)
                    cut = rows[:, j0:j1, 0:F]
                    if l == 1:
                        weight = logit[:, bass.ds(i * RING + j0, n), :]
                        V.tensor_tensor(cut.rearrange("p j (h c) -> p j h c", h=H),
                                        cut.rearrange("p j (h c) -> p j h c", h=H),
                                        weight.unsqueeze(3).to_broadcast([P, n, H, F // H]), ALU.mult)
                        V.tensor_scalar(rows[:, j0:j1, F:F + H], weight, 1.0, None, ALU.mult).then_inc(s_scaled, 1)
                    else:
                        V.tensor_tensor(cut, cut, slots[q][:, bass.ds(i * RING + j0, n), 3:4].to_broadcast([P, n, F]),
                                        ALU.mult).then_inc(s_scaled, 1)

                def add_up(i, g, ahead=None):
                    j0, j1 = PARTS[g]
                    tiles = i * RING + l * NT
                    _, buckets = nc.values_load_multi_w_load_instructions(
                        tile_bucket_i[q][0:1, bass.ds(i * RING + j0, j1 - j0)], engines=[mybir.EngineType.DVE],
                        min_val=0, max_val=NB - 1,
                        skip_runtime_bounds_check_because="a count of bucket starts less one, at most NB - 1")
                    for j in range(j0, j1):
                        dve.wait_ge(s_mm, tiles + (j + 1))
                        dve.wait_ge(s_added, tiles + (j + RING))
                        acc = into[:, bass.ds(buckets[j - j0], 1), 0:width]
                        V.tensor_tensor(acc, acc, ps[:, j % BLK:j % BLK + 1, 0:width], ALU.add).then_inc(s_added, 1)
                        if ahead:
                            one_onehot(*ahead, PARTS[ahead[1]][0] + j - j0)

                if l > 0:
                    for u in range(2):
                        dve.wait_ge(s_store[u], stored(l * PITERS, u) * 16)
                for g in range(2):
                    for j in range(*PARTS[g]):
                        one_onehot(0, g, j)
                weigh(0, 0)
                with dve.Fori(0, ITERS - 1) as i:
                    for g in range(NPART):
                        weigh(i + (g + 1) // NPART, (g + 1) % NPART)
                        add_up(i, g, (i + (g + 2) // NPART, (g + 2) % NPART))
                for g in range(NPART):
                    if g + 1 < NPART:
                        weigh(ITERS - 1, g + 1)
                    add_up(ITERS - 1, g, (ITERS - 1, g + 2) if g + 2 < NPART else None)
                dve.wait_ge(s_added, (l + 1) * NT + RING)

            def take_rows(l, g):
                group = (l - 1) * PITERS + g
                u = group % 2
                if group > 1:
                    dve.wait_ge(s_store[u], stored(group, u) * 16)
                for j in range(NG):
                    n = g * NG + j
                    bank = (4 + j) % 8
                    wide = FW if l == 3 else F
                    dve.wait_ge(s_row, group * NG + j + 1 + NG)
                    if l in (1, 3):
                        V.tensor_copy(attn[:, n, :], ps[:, bank, F:FW]).then_inc(s_att, 1)
                    V.tensor_copy(row_ring[:, u * NG + j, 0:wide], ps[:, bank, 0:wide]).then_inc(s_row_out, 1)

            def fold(W, A, order):
                for c, a in enumerate(order):
                    for k in range(KT):
                        step(V.tensor_tensor(folded, W[:, k, 0:F], A[:, a, :], ALU.mult))
                        step(V.reduce_sum(W[:, k, F + c * H:F + (c + 1) * H], folded.rearrange("p (h c) -> p h c", h=H),
                                          axis=AX.X))

            dve.wait_ge(s_cst, 16)
            V.tensor_scalar(below_b[:, :], slot_no[:, 0:ET], part, None, ALU.is_gt).then_inc(s_constb, 1)
            V.memset(rec_s[:, :, 1], 0.0).then_inc(s_rec_s, 1)
            dve.wait_ge(s_src, 16)
            mark_members(1).then_inc(s_member, 1)
            dve.wait_ge(s_in, 4 * 16)
            step(V.tensor_tensor(rank_f[:, :], row_dst, row_next, ALU.subtract))
            V.reduce_max(worst[:, 0:1], rank_f[:, :], axis=AX.X).then_inc(s_worst, 1)
            take_counts(1)
            place_buckets(1)
            dve.wait_ge(s_x, 16)
            norm_stats(0, 0, 1)
            rank_edges(1, 0)
            norm_stats(0, 1, PITERS)
            rank_edges(1, 1)
            spread_buckets(1)
            step(V.tensor_scalar_min(rec_d[:, 0:ET, 1], ecol[:, 0, :], float(NB * P - 1)))
            V.scalar_tensor_tensor(out=rec_d[:, 0:ET, 0], in0=rec_d[:, 0:ET, 1], scalar=float(R), in1=ecol[:, 2, :],
                                   op0=ALU.mult, op1=ALU.add).then_inc(s_rec_d, 1)
            mark_members(0).then_inc(s_member, 1)
            take_counts(0)
            place_buckets(0)
            spread_buckets(0)
            dve.wait_ge(s_w, 112)
            fold(W1, A1, (0, 1))
            fold(W3, A3, (1, 0))
            step(V.tensor_scalar(tmp_j[:, 0:NB], ecol[:, 0, 0:NB], 7, None, ALU.arith_shift_right))
            step(V.tensor_copy(last_hi[:, 0, :], tmp_j[:, 0:NB]))
            step(V.scalar_tensor_tensor(out=last_lo[:, :], in0=last_hi[:, 0, :], scalar=-float(P), in1=ecol[:, 0, 0:NB],
                                        op0=ALU.mult, op1=ALU.add))
            V.tensor_tensor(last_pick[:, :, :], iota[:, 0:NB].unsqueeze(1).to_broadcast([P, NB, NB]),
                            last_hi[:, 0, :].unsqueeze(2).to_broadcast([P, NB, NB]), ALU.is_equal).then_inc(s_last_lo, 1)
            _, (is_unsorted,) = nc.values_load_multi_w_load_instructions(
                unsorted_i[0:1, 0:1], engines=[mybir.EngineType.DVE], min_val=0, max_val=1,
                skip_runtime_bounds_check_because="the result of a comparison")
            with dve.If(is_unsorted):
                rank_edges(0, 0)
                rank_edges(0, 1)
            localise(0)
            step(V.tensor_copy(tmp_i[:, :], slots[0][:, :, 1]))
            step(V.tensor_scalar(tmp_i[:, :], tmp_i[:, :], 7, None, ALU.arith_shift_right))
            step(V.tensor_copy(hi_f[:, 0, :], tmp_i[:, :]))
            step(V.tensor_copy(hi_b[:, :], tmp_i[:, :]))
            step(V.scalar_tensor_tensor(out=lo_b[:, 0, :], in0=hi_f[:, 0, :], scalar=-float(P), in1=slots[0][:, :, 1],
                                        op0=ALU.mult, op1=ALU.add))
            V.tensor_scalar(lo_b[:, 1, :], local[0][:, :], -1.0, float(P), ALU.max, ALU.min).then_inc(s_lo, 1)
            dve.wait_ge(s_lo_mm, 1)
            for s in range(2):
                V.tensor_copy(lo_T[:, s, 0:CH - 1, :].rearrange("p c n -> p (c n)"),
                              ps[:, s, 0:(CH - 1) * P]).then_inc(s_lo_out, 1)
                V.tensor_copy(lo_T[0:TLAST, s, CH - 1, :], ps[0:TLAST, s, (CH - 1) * P:CH * P]).then_inc(s_lo_out, 1)
            V.tensor_copy(last_T[:, :], ps[0:NB, 2, 0:P]).then_inc(s_lo_out, 1)
            step(V.tensor_scalar(off[:, :], local[0][:, :], 0.0, None, ALU.is_ge))
            step(V.scalar_tensor_tensor(out=off[:, :], in0=local[0][:, :], scalar=float(P), in1=off[:, :],
                                        op0=ALU.is_lt, op1=ALU.mult))
            step(V.tensor_scalar(off[:, :], off[:, :], FAR, -FAR, ALU.mult, ALU.add))
            dve.wait_ge(s_h, NB)
            step(V.tensor_add(X[:, :, :], X[:, :, :], bias0_b[:, :].unsqueeze(1).to_broadcast([P, NB, F])))
            aggregate(0, 0)

            norm_stats(1, 0, 1)
            step(V.memset(pick[:, NB:PK, :], 1.0))
            for g in range(PITERS):
                if g + 1 < PITERS:
                    norm_stats(1, g + 1, g + 2)
                for b in range(g * NG, (g + 1) * NG):
                    V.tensor_scalar(pick[:, b, :], hi_b[:, :], float(b), None, ALU.is_equal)
                take_rows(1, g)
            dve.wait_ge(s_att, NB)
            rest = attn_rest[:, :, :, :]
            step(V.tensor_copy(rest, attn[:, :, :].rearrange("p n (s h) -> p s n h", s=2)))
            for c in range(3):
                step(V.tensor_copy(attn_part[:, c, :, :], rest[:, 0, :, :]))
                step(V.tensor_copy(attn_part_d[:, :, c, :], rest[:, 1, :, :]))
                step(V.tensor_sub(rest[:, 0, :, :], rest[:, 0, :, :], attn_part[:, c, :, :]))
                step(V.tensor_sub(rest[:, 1, :, :], rest[:, 1, :, :], attn_part_d[:, :, c, :]))
            dve.sem_inc(s_parts, 1)

            def transposed_onehots(i, k):
                dve.wait_ge(s_numbers[k], i * 16 + 16)
                dve.wait_ge(s_picked_mm, i * SETS + (k + 1))
                V.tensor_scalar(onehotT[k][:, wide_T:2 * wide_T], numbers[:, k, 1, :],
                                part, None, ALU.is_equal).then_inc(s_onehots_dst, 1)

            def choose(i, k):
                hold(dve, s_picked_mm, i * SETS + (k + 1 + SETS), s_tok_dve)
                grid = ps[:, 2 * k:2 * k + 2, :].rearrange("p b (j c) -> p (b j) c", c=P)[:, 0:BLK, 0:PK * H]
                V.tensor_tensor(picked[k].rearrange("p j (a h) -> p j a h", h=H), grid.rearrange("p j (a h) -> p j a h", h=H),
                                pick[:, :, bass.ds(i * RING + k * BLK, BLK)].rearrange("p b j -> p j b").unsqueeze(3).to_broadcast(
                                    [P, BLK, PK, H]), ALU.mult).then_inc(s_pick, 1)

            def sum_choice(i, k):
                hold(dve, s_pick, i * SETS + (k + 1), s_tok_dve)
                V.reduce_sum(logit[:, bass.ds(i * RING + k * BLK, BLK), :], picked[k].rearrange("p j (a h) -> p j h a", h=H),
                             axis=AX.X).then_inc(s_picked, 1)

            transposed_onehots(0, 0)
            transposed_onehots(0, 1)
            with dve.Fori(0, ITERS - 1) as i:
                for k in range(SETS):
                    choose(i, k)
                    transposed_onehots(i + (k + 2) // SETS, (k + 2) % SETS)
                    sum_choice(i, k)
            for k in range(SETS):
                choose(ITERS - 1, k)
                if k + 2 < SETS:
                    transposed_onehots(ITERS - 1, k + 2)
                sum_choice(ITERS - 1, k)
            dve.wait_ge(s_picked, ITERS * SETS + SETS)
            step(V.scalar_tensor_tensor(out=logit, in0=logit, scalar=0.2, in1=logit, op0=ALU.mult, op1=ALU.max))
            step(V.tensor_tensor(logit, logit, slots[0][:, :, 3:4].to_broadcast([P, NT, H]), ALU.mult))
            step(V.tensor_tensor(logit, logit, off[:, :].unsqueeze(2).to_broadcast([P, NT, H]), ALU.add))
            V.reduce_max(mx[:, 0:1], logit.rearrange("p t h -> p (t h)"), axis=AX.X).then_inc(s_mx, 1)
            dve.wait_ge(s_mT, 1)
            step(V.reduce_max(mrow[0:1, 0:1], ps[0:1, 0, 0:P], axis=AX.X))
            V.tensor_scalar_mul(mrow[0:1, 1:2], mrow[0:1, 0:1], -1.0).then_inc(s_m1, 1)
            dve.wait_ge(s_mB, 1)
            V.tensor_copy(mx[:, 1:2], ps[:, 1, 0:1]).then_inc(s_negM, 1)
            dve.wait_ge(s_exp, 1)
            dve.wait_ge(s_zero, 1)
            aggregate(1, 0)
            step(V.tensor_scalar_add(sc[:, :, :], U[:, :, F:F + H], 1e-10))
            step(V.reciprocal(sc[:, :, :], sc[:, :, :]))

            def add_sums(g):
                group = slice(g * NG, (g + 1) * NG)
                for h in range(H):
                    cut = U[:, group, h * (F // H):(h + 1) * (F // H)]
                    last = V.tensor_tensor(cut, cut, sc[:, group, h:h + 1].to_broadcast([P, NG, F // H]), ALU.mult)
                step(last)
                step(V.tensor_add(X[:, group, :], X[:, group, :], U[:, group, 0:F]))

            add_sums(0)
            norm_stats(2, 0, 1)
            for g in range(PITERS):
                if g + 1 < PITERS:
                    add_sums(g + 1)
                    norm_stats(2, g + 1, g + 2)
                take_rows(2, g)
            localise(1)
            dve.wait_ge(s_h, 3 * NB)
            step(V.tensor_add(X[:, :, :], X[:, :, :], b2_b[:, :].unsqueeze(1).to_broadcast([P, NB, F])))
            aggregate(2, 1)
            dve.wait_ge(s_last_numbers, 16)

            norm_stats(3, 0, 1)
            for g in range(PITERS):
                if g + 1 < PITERS:
                    norm_stats(3, g + 1, g + 2)
                if g == 0:
                    V.tensor_scalar(last_onehots, last_numbers, part, None, ALU.is_equal).then_inc(s_last_onehots, 1)
                take_rows(3, g)
            dve.wait_ge(s_att, 2 * NB)
            rest = attn_rest[:, 0, :, :]
            step(V.tensor_copy(rest, attn[:, :, H:2 * H]))
            for c in range(3):
                step(V.tensor_copy(attn_part[:, c, :, :], rest))
                step(V.tensor_sub(rest, rest, attn_part[:, c, :, :]))
            dve.sem_inc(s_last_parts, 1)
            dve.wait_ge(s_last_picked, 1)
            grid = ps[:, 0:(NB + 3) // 4, :].rearrange("p b (j c) -> p (b j) c", c=P)[:, 0:NB, 0:NB * H]
            step(V.tensor_tensor(last_chosen.rearrange("p j (a h) -> p j a h", h=H), grid.rearrange("p j (a h) -> p j a h", h=H),
                                 last_pick[:, :, :].unsqueeze(3).to_broadcast([P, NB, NB, H]), ALU.mult))
            step(V.reduce_sum(al[:, :, :], last_chosen.rearrange("p j (a h) -> p j h a", h=H), axis=AX.X))
            for g in range(PITERS):
                cut = slice(g * NG, (g + 1) * NG)
                s, e = sc[:, cut, :], sc2[:, cut, :]
                top, whole = sm[:, cut, 0], sm[:, cut, 1]
                dve.wait_ge(s_last[g], NG * 16)
                step(V.tensor_add(s, al[:, cut, :], final_rows[:, cut, F:F + H]))
                step(V.scalar_tensor_tensor(out=s, in0=s, scalar=0.01, in1=s, op0=ALU.mult, op1=ALU.max))
                step(V.reduce_max(top, s, axis=AX.X))
                V.tensor_tensor(s, s, sm[:, cut, 0:1].to_broadcast([P, NG, H]), ALU.subtract).then_inc(s_e3, 1)
                dve.wait_ge(s_e3x, g + 1)
                step(V.reduce_sum(whole, e, axis=AX.X))
                step(V.reciprocal(whole, whole))
                step(V.tensor_tensor(e, e, sm[:, cut, 1:2].to_broadcast([P, NG, H]), ALU.mult))
                heads = final_rows[:, cut, 0:F].rearrange("p n (h c) -> p n h c", h=H)
                mixed = h_ring[:, :, 0:F // H]
                step(V.tensor_tensor(heads, heads, e.unsqueeze(3).to_broadcast([P, NG, H, F // H]), ALU.mult))
                step(V.reduce_sum(mixed, heads.rearrange("p n h c -> p n c h"), axis=AX.X))
                nodes = X[:, cut, :].rearrange("p n (h c) -> p n h c", h=H)
                V.tensor_tensor(nodes, nodes, mixed.unsqueeze(2).to_broadcast([P, NG, H, F // H]), ALU.add).then_inc(s_done, 1)

        @block.tensor
        def _(pe):
            mm = nc.tensor.matmul
            pe.sem_inc(s_tr, NG)
            pe.sem_inc(s_quarter, 4 * NG)
            pe.sem_inc(s_row, NG)
            pe.sem_inc(s_picked_mm, SETS)

            def count_edges(c, chunk):
                pe.wait_ge(s_member, c + 1)
                if c:
                    pe.wait_ge(s_spread_out, c)
                wide = P if chunk < CH - 1 else CLAST
                for b in range(NB):
                    last = mm(ps[0:wide, 0, chunk * NB + b:chunk * NB + b + 1], member[:, b, chunk * P:chunk * P + wide],
                              ones_b[:, 0:1], start=True, stop=True)
                if chunk == CH - 1:
                    last.then_inc(s_count, 1)

            def size_buckets(c):
                pe.wait_ge(s_count_out, 2 * c + 2)
                for chunk in range(CH):
                    wide = P if chunk < CH - 1 else CLAST
                    last = mm(ps[:, 1, 0:NB], ones_b[0:wide, :], count_b[0:wide, chunk, :], start=(chunk == 0),
                              stop=(chunk == CH - 1))
                last.then_inc(s_size, 1)

            def rank_bucket(c, m):
                half, b = m // NB, m % NB
                if m < 2:
                    pe.wait_ge(s_sizes, c + 1)
                    if c:
                        pe.wait_ge(s_spread_out, c + 1)
                else:
                    pe.wait_ge(s_ranked, c * 2 * NB + m - 1)
                t0, t1 = HALVES[half]
                mm(ps[:, m % 2, t0:t1], below_b[:, 0:P], member[:, b, t0:t1], start=True, stop=False)
                chunks = [chunk for chunk in range(CH) if chunk * P < t1]
                for chunk in chunks:
                    deep = P if chunk < CH - 1 else CLAST
                    first = max(t0, chunk * P)
                    last = mm(ps[:, m % 2, first:t1], count_b[0:deep, chunk, b:b + 1].to_broadcast([deep, P]),
                              below_b[0:deep, first - chunk * P:t1 - chunk * P], start=False, stop=(chunk == chunks[-1]))
                last.then_inc(s_rank, 1)

            def turn_starts(c):
                pe.wait_ge(s_sizes, c + 1)
                if c == 0:
                    pe.wait_ge(s_ranked, 2 * NB)
                nc.tensor.transpose(ps[0:NB, 0, 0:P], total[:, 1 - c, 3, :], ident).then_inc(s_spread, 1)

            def sum_begun(c):
                pe.wait_ge(s_begun, c + 1)
                mm(ps[:, 0, 0:NT], ones_row[0:NB, 0:P], begun[:, :], start=True, stop=True).then_inc(s_spread, 1)

            def beside(n):
                if n < 13:
                    for m in range(NB + 2 * n, min(NB + 2 * n + 2, 2 * NB)):
                        rank_bucket(0, m)
                elif n == 15:
                    turn_starts(0)
                elif n == 17:
                    sum_begun(0)
                elif 26 <= n < 26 + CH:
                    count_edges(1, n - 26)
                elif n == 31:
                    size_buckets(1)
                elif n == 36:
                    turn_starts(1)
                elif n == 38:
                    sum_begun(1)

            def project(l, start, end, counting=False):
                c0 = l * NB
                W = (W0, W1, W2, W3)[l]
                wide = (2 * F, FW, F, FW)[l]

                def transpose(i, j):
                    pe.wait_ge(s_h, i * NG + (c0 + j + 1))
                    pe.wait_ge(s_hT, i * NG + (c0 + j + 1))
                    for k in range(KT):
                        last = nc.tensor.transpose(ps[:, 2 + j % 2, k * P:(k + 1) * P], h_ring[:, j, k * P:(k + 1) * P], ident)
                    last.then_inc(s_tr, 1)

                def products(i, j):
                    pe.wait_ge(s_hT, i * NG + (c0 + j + 2))
                    if l == 0:
                        for q in range(4):
                            pe.wait_ge(s_quarter_out, i * (4 * NG) + (4 * j + q + 1))
                            for k in range(KT):
                                last = mm(ps[:, 4 + q, :], hT_ring[:, j, k, :], W[:, k, q * wide:(q + 1) * wide],
                                          start=(k == 0), stop=(k == KT - 1))
                            last.then_inc(s_quarter, 1)
                            if counting:
                                beside(((start - 1) * NG + j) * 4 + q)
                    else:
                        bank = (4 + j) % 8
                        pe.wait_ge(s_row_out, i * NG + ((l - 1) * NB + j + 1))
                        for k in range(KT):
                            last = mm(ps[:, bank, 0:wide], hT_ring[:, j, k, :], W[:, k, :], start=(k == 0), stop=(k == KT - 1))
                        last.then_inc(s_row, 1)

                with pe.Fori(start, end) as i:
                    transpose(i, 0)
                    transpose(i, 1)
                    for j in range(NG):
                        products(i, j)
                        if j + 2 < NG:
                            transpose(i, j + 2)

            def aggregate(l):
                with pe.Fori(0, ITERS) as i:
                    for g in range(NPART):
                        tiles = i * RING + l * NT
                        j0, j1 = PARTS[g]
                        pe.wait_ge(s_onehot, i * NPART + (l * ITERS * NPART + g + 1))
                        if l == 0:
                            pe.wait_ge(s_rows[g], i * ((j1 - j0) * 16) + (j1 - j0) * 16)
                        else:
                            pe.wait_ge(s_scaled, i * NPART + ((l - 1) * ITERS * NPART + g + 1))
                        for j in range(j0, j1):
                            pe.wait_ge(s_added, tiles + (j + 1 - BLK + RING))
                            width = F + H if l == 1 else F
                            mm(ps[:, j % BLK, 0:width], onehot[:, j, :], rows[:, j, 0:width],
                               start=True, stop=True).then_inc(s_mm, 1)

            pe.wait_ge(s_constb, 3)
            for chunk in range(CH):
                count_edges(0, chunk)
            size_buckets(0)
            for m in range(NB):
                rank_bucket(0, m)
            pe.wait_ge(s_w0, 16)
            project(0, 0, 1)
            for turn in (1, 2):
                project(0, turn, turn + 1, counting=True)
            project(0, 3, PITERS)
            pe.wait_ge(s_sizes, 2)
            pe.sem_inc(s_tok_pe, 1)
            _, (is_unsorted,) = nc.values_load_multi_w_load_instructions(
                unsorted_i[0:1, 0:1], engines=[mybir.EngineType.PE], min_val=0, max_val=1,
                skip_runtime_bounds_check_because="the result of a comparison")
            with pe.If(is_unsorted):
                for m in range(2 * NB):
                    rank_bucket(1, m)
            pe.wait_ge(s_lo, 1)
            pe.wait_ge(s_spread_out, 2)
            for s in range(2):
                for chunk in range(CH):
                    wide = P if chunk < CH - 1 else TLAST
                    mm(ps[0:wide, s, chunk * P:(chunk + 1) * P], lo_b[:, s, chunk * P:chunk * P + wide],
                              ident_b[:, :], start=True, stop=True)
            pe.wait_ge(s_last_lo, 1)
            mm(ps[0:NB, 2, 0:P], last_lo[:, :], ident_b[:, :], start=True, stop=True).then_inc(s_lo_mm, 1)
            pe.wait_ge(s_lo_out, 5)
            aggregate(0)
            pe.wait_ge(s_w, 112)
            project(1, 0, PITERS)
            pe.wait_ge(s_parts, 1)

            def look_up(i, k):
                _, buckets = nc.values_load_multi_w_load_instructions(
                    tile_bucket_i[0][0:1, bass.ds(i * RING + k * BLK, BLK)], engines=[mybir.EngineType.PE],
                    min_val=0, max_val=NB - 1,
                    skip_runtime_bounds_check_because="a count of bucket starts less one, at most NB - 1")
                pe.wait_ge(s_onehots_src, i * SETS + (k + 1 + SETS))
                pe.wait_ge(s_onehots_dst, i * SETS + (k + 1 + SETS))
                pe.wait_ge(s_picked, i * SETS + (k + 1))
                for j in range(BLK):
                    at = (j % 4) * P
                    for c in range(3):
                        mm(ps[:, 2 * k + j // 4, at:at + NB * H], onehotT[k][:, j * P:(j + 1) * P],
                           attn_part[:, c, :, :].rearrange("p n h -> p (n h)"), start=(c == 0), stop=(c == 2))
                    last = mm(ps[:, 2 * k + j // 4, at + NB * H:at + PK * H],
                              onehotT[k][:, wide_T + j * P:wide_T + (j + 1) * P],
                              attn_part_d[:, bass.ds(buckets[j], 1), :, :].rearrange("p n c h -> p (n c h)"),
                              start=True, stop=True)
                last.then_inc(s_picked_mm, 1)

            with pe.Fori(0, ITERS) as i:
                for k in range(SETS):
                    look_up(i, k)
            pe.wait_ge(s_mx, 1)
            nc.tensor.transpose(ps[0:1, 0, 0:P], mx[:, 0:1], ident).then_inc(s_mT, 1)
            pe.wait_ge(s_m1, 1)
            mm(ps[:, 1, 0:1], ones_row[0:1, 0:P], mrow[0:1, 1:2], start=True, stop=True).then_inc(s_mB, 1)
            aggregate(1)
            project(2, 0, PITERS)
            aggregate(2)
            project(3, 0, PITERS)
            pe.wait_ge(s_last_onehots, 1)
            pe.wait_ge(s_last_parts, 1)
            for t in range(NB):
                for c in range(3):
                    last = mm(ps[:, t // 4, (t % 4) * P:(t % 4) * P + NB * H], last_onehots[:, t * P:(t + 1) * P],
                              attn_part[:, c, :, :].rearrange("p n h -> p (n h)"), start=(c == 0), stop=(c == 2))
            last.then_inc(s_last_picked, 1)


_OUT = ((P, NB, F), "float32")


def kernel(**inputs):
    import numpy as np
    import concourse.bacc as bacc
    from concourse.bass_utils import run_bass_kernel_spmd as run

    def nodes(a):
        a = np.pad(np.asarray(a), ((0, NB * P - N), (0, 0)))
        return a.reshape(NB, P, F).transpose(1, 0, 2)

    def edges(a, fill):
        a = np.pad(np.asarray(a), (0, ET * P - E), constant_values=fill)
        return a.reshape(ET, P).T

    def deep(a):
        return np.asarray(a).reshape(KT, P, -1).transpose(1, 0, 2)

    consts = np.zeros((P, CW), np.float32)
    consts[:, C_IOTA:C_IOTA + P] = np.arange(P)
    consts[:, C_ID:C_ID + P] = np.eye(P)
    consts[:, C_SLOT:C_SLOT + NT] = np.arange(NT)
    consts[:, C_PART] = np.arange(P)
    consts[:, C_MINUS] = -np.arange(P)
    left = E - (ET - 1) * P
    consts[left:, C_PAD] = P * NT + np.arange(left, P)

    def edges_by_row(a, ahead):
        return np.pad(np.asarray(a)[ahead:], (0, ET * P - E + ahead), constant_values=NB * P).reshape(P, ET)

    src, dst, kind = inputs["src"], inputs["dst"], inputs["edge_type_8"]
    arrays = {
        "x": nodes(inputs["x"]),
        "ecols": np.stack([edges(src, NB * P), edges(dst, NB * P), edges(kind, 0)], 1),
        "wcols": edges(inputs["edge_weight"], 0),
        "erows": np.stack([edges_by_row(dst, 0), edges_by_row(dst, 1)], 1),
        "consts": consts,
        "w0": deep(np.asarray(inputs["L0_gnn_weight"]).transpose(2, 0, 1).reshape(F, R * F)),
        "bias0": np.asarray(inputs["L0_gnn_bias"]).reshape(1, F),
        "w1": deep(np.asarray(inputs["L1_gnn_W"]).transpose(1, 0, 2).reshape(F, F)),
        "a1": np.stack([np.asarray(inputs["L1_gnn_a_src"]).reshape(F), np.asarray(inputs["L1_gnn_a_dst"]).reshape(F)]),
        "w2": deep(inputs["L2_gnn_W"]),
        "b2": np.asarray(inputs["L2_gnn_b"]).reshape(1, F),
        "w3": deep(inputs["L3_gnn_weight"]),
        "a3": np.stack([np.asarray(inputs["L3_gnn_attn_l"]).reshape(F), np.asarray(inputs["L3_gnn_attn_r"]).reshape(F)]),
    }
    nc = bacc.Bacc("TRN2", target_bir_lowering=False, num_devices=1)
    maps, args = {}, []
    for name, a in arrays.items():
        a = np.ascontiguousarray(a)
        maps[f"in_{name}"] = a
        args.append(nc.dram_tensor(f"in_{name}", a.shape, mybir.dt.from_np(a.dtype), kind="ExternalInput").ap())
    o = nc.dram_tensor("out_0", _OUT[0], F32, kind="ExternalOutput").ap()
    build(nc, *args, o)
    r = run(nc, [maps], core_ids=[0])
    got = r.results[0]["out_0"]
    return np.ascontiguousarray(got.transpose(1, 0, 2).reshape(NB * P, F)[:N])
```
